# Optimizing a Trainium2 kernel written in Bass

```python
import numpy as np
import jax
import jax.numpy as jnp

def _softmax(x, axis=-1):
    return jax.nn.softmax(x, axis=axis)

def _gelu(x):
    return jax.nn.gelu(x, approximate=True)

def _silu(x):
    return jax.nn.silu(x)

def _sigmoid(x):
    return jax.nn.sigmoid(x)

def _layernorm(x, axis=-1, eps=1e-05):
    m = jnp.mean(x, axis=axis, keepdims=True)
    v = jnp.var(x, axis=axis, keepdims=True)
    return (x - m) / jnp.sqrt(v + eps)

def _scatter_add(tgt, idx, src, axis=0):
    return tgt.at[idx].add(src)

def _segment_sum(src, seg, n):
    return jax.ops.segment_sum(src, seg, n)
kernel_name = 'mk_flamingo_gated_d1_seqx_r4_ea8c8d'

def setup_inputs(seed: int=0):
    np.random.seed(seed)
    _w = jnp.asarray

    def _rec_inputs():
        import jax
        import jax.numpy as jnp
        _rk = jax.random.key(seed)
        x = -0.000125 + 0.9999 * jax.random.normal(jax.random.fold_in(_rk, 1), (8, 256, 1024), jnp.float32)
        _lenS = 256 - jax.random.randint(jax.random.fold_in(_rk, 7), (8,), 0, max(1, 256 // 4) + 1, jnp.int32)
        _lenS2 = 256 - jax.random.randint(jax.random.fold_in(_rk, 8), (8,), 0, max(1, 256 // 4) + 1, jnp.int32)
        _ctx_4096P = jax.random.normal(jax.random.fold_in(_rk, 11), (8, 16, 1024), jnp.float32)
        _ctx_4096c = jax.random.dirichlet(jax.random.fold_in(_rk, 511), 0.3 * jnp.ones((16,), jnp.float32), (8, 256))
        _ctx_4096t = jnp.einsum('bsk,bkd->bsd', _ctx_4096c, _ctx_4096P)
        _ctx_4096t = _ctx_4096t * jax.lax.rsqrt(jnp.mean(jnp.square(_ctx_4096t)) + 1e-12) * 0.953939
        ctx_4096 = -1.52775e-05 + 0.999936 * (_ctx_4096t + 0.3 * jax.random.normal(jax.random.fold_in(_rk, 611), (8, 256, 1024), jnp.float32))
        _g = jax.random.normal(jax.random.fold_in(_rk, 9001), (2, 1), jnp.float32)
        _g = jnp.sign(_g) * jnp.maximum(jnp.abs(_g), 1.0) + (_g == 0) * 1.0
        g_xattn = _g[0]
        g_ffn = _g[1]
        return (x, ctx_4096, g_xattn, g_ffn)
    x, ctx_4096, g_xattn, g_ffn = _rec_inputs()

    def _L0_xattn_setup():
        import jax, jax.numpy as jnp
        import numpy as np
        H = 8
        C = 2

        def _autocorrelation(Q, K, V):
            B, L, D = Q.shape
            d = D // H
            q = Q.reshape(B, L, H, d).transpose(0, 2, 1, 3)
            k = K.reshape(B, L, H, d).transpose(0, 2, 1, 3)
            v = V.reshape(B, L, H, d).transpose(0, 2, 1, 3)
            qf = jnp.fft.fft(q, axis=2)
            kf = jnp.fft.fft(k, axis=2)
            corr = jnp.fft.ifft(qf * jnp.conj(kf), axis=2).real
            topk = int(C * np.log(L))
            w, idx = jax.lax.top_k(corr.transpose(0, 1, 3, 2), topk)
            w = jax.nn.softmax(w, axis=-1)
            pos = jnp.arange(L)[:, None]
            out = jnp.zeros_like(v)
            for i in range(topk):
                g = jnp.minimum(idx[:, :, None, :, i] + pos, L - 1)
                out = out + w[:, :, None, :, i] * jnp.take_along_axis(v, g, axis=2)
            return out.transpose(0, 2, 1, 3).reshape(B, L, D)
        key = jax.random.key(seed)
        k1, k2, k3 = jax.random.split(key, 3)
        B, L, D = (16, 128, 1024)
        Q = jax.random.normal(k1, (B, L, D), dtype=jnp.float32)
        K = jax.random.normal(k2, (B, L, D), dtype=jnp.float32)
        V = jax.random.normal(k3, (B, L, D), dtype=jnp.float32)
        return {'Q': Q, 'K': K, 'V': V}
    _L0_xattn_all = _L0_xattn_setup()
    _L0_xattn_in = {k: v for k, v in _L0_xattn_all.items() if k in ()}
    del _L0_xattn_all

    def _L0_ffn_setup():
        import jax, jax.numpy as jnp
        import numpy as np
        EPS = 1e-06
        QMAX = 127.0

        def _quant_act(x):
            s = jnp.max(jnp.abs(x), axis=-1, keepdims=True) / QMAX
            s = jnp.maximum(s, 1e-08)
            q = jnp.clip(jnp.round(x / s), -QMAX, QMAX)
            return (q, s)

        def _quant_w(W):
            ws = jnp.max(jnp.abs(W), axis=1, keepdims=True) / QMAX
            ws = jnp.maximum(ws, 1e-08)
            Wq = jnp.clip(jnp.round(W / ws), -QMAX, QMAX)
            return (Wq, ws)
        key = jax.random.key(seed)
        k1, k2, k3, k4, k5 = jax.random.split(key, 5)
        B, S, D, I = (4, 512, 1024, 2752)
        return {'hidden_states': jax.random.normal(k1, (B, S, D), dtype=jnp.float32), 'rmsnorm_weight': jax.random.uniform(k2, (D,), dtype=jnp.float32), 'Wg': jax.random.normal(k3, (I, D), dtype=jnp.float32) * 0.02, 'Wu': jax.random.normal(k4, (I, D), dtype=jnp.float32) * 0.02, 'Wd': jax.random.normal(k5, (D, I), dtype=jnp.float32) * 0.02}
    _L0_ffn_all = _L0_ffn_setup()
    _L0_ffn_in = {k: v for k, v in _L0_ffn_all.items() if k in ('rmsnorm_weight', 'Wg', 'Wu', 'Wd')}
    del _L0_ffn_all
    return {'x': x, 'ctx_4096': ctx_4096, 'g_xattn': g_xattn, 'g_ffn': g_ffn, 'L0_ffn_rmsnorm_weight': _L0_ffn_in['rmsnorm_weight'], 'L0_ffn_Wg': _L0_ffn_in['Wg'], 'L0_ffn_Wu': _L0_ffn_in['Wu'], 'L0_ffn_Wd': _L0_ffn_in['Wd']}

def reference(x, ctx_4096, g_xattn, g_ffn, L0_ffn_rmsnorm_weight, L0_ffn_Wg, L0_ffn_Wu, L0_ffn_Wd):
    import jax
    import jax.numpy as jnp

    def _L0_xattn_ref(Q, K, V):
        import jax, jax.numpy as jnp
        import numpy as np
        H = 8
        C = 2

        def _autocorrelation(Q, K, V):
            B, L, D = Q.shape
            d = D // H
            q = Q.reshape(B, L, H, d).transpose(0, 2, 1, 3)
            k = K.reshape(B, L, H, d).transpose(0, 2, 1, 3)
            v = V.reshape(B, L, H, d).transpose(0, 2, 1, 3)
            qf = jnp.fft.fft(q, axis=2)
            kf = jnp.fft.fft(k, axis=2)
            corr = jnp.fft.ifft(qf * jnp.conj(kf), axis=2).real
            topk = int(C * np.log(L))
            w, idx = jax.lax.top_k(corr.transpose(0, 1, 3, 2), topk)
            w = jax.nn.softmax(w, axis=-1)
            pos = jnp.arange(L)[:, None]
            out = jnp.zeros_like(v)
            for i in range(topk):
                g = jnp.minimum(idx[:, :, None, :, i] + pos, L - 1)
                out = out + w[:, :, None, :, i] * jnp.take_along_axis(v, g, axis=2)
            return out.transpose(0, 2, 1, 3).reshape(B, L, D)
        return _autocorrelation(Q, K, V)

    def _L0_ffn_ref(hidden_states, rmsnorm_weight, Wg, Wu, Wd):
        import jax, jax.numpy as jnp
        import numpy as np
        EPS = 1e-06
        QMAX = 127.0

        def _quant_act(x):
            s = jnp.max(jnp.abs(x), axis=-1, keepdims=True) / QMAX
            s = jnp.maximum(s, 1e-08)
            q = jnp.clip(jnp.round(x / s), -QMAX, QMAX)
            return (q, s)

        def _quant_w(W):
            ws = jnp.max(jnp.abs(W), axis=1, keepdims=True) / QMAX
            ws = jnp.maximum(ws, 1e-08)
            Wq = jnp.clip(jnp.round(W / ws), -QMAX, QMAX)
            return (Wq, ws)
        B, S, D = hidden_states.shape
        x = hidden_states.reshape(B * S, D)
        x = x * jax.lax.rsqrt(jnp.mean(x * x, axis=-1, keepdims=True) + EPS)
        x = x * rmsnorm_weight
        q, s = _quant_act(x)
        Wgq, wsg = _quant_w(Wg)
        Wuq, wsu = _quant_w(Wu)
        gate = jnp.einsum('td,id->ti', q, Wgq) * s * wsg.T
        up = jnp.einsum('td,id->ti', q, Wuq) * s * wsu.T
        h = jax.nn.silu(gate) * up
        q2, s2 = _quant_act(h)
        Wdq, wsd = _quant_w(Wd)
        out = jnp.einsum('ti,di->td', q2, Wdq) * s2 * wsd.T
        return out.reshape(B, S, D)
    x = x + jnp.tanh(g_xattn[0]) * _L0_xattn_ref(_layernorm(x, axis=-1), ctx_4096, ctx_4096)
    x = x + jnp.tanh(g_ffn[0]) * _L0_ffn_ref(_layernorm(x, axis=-1), L0_ffn_rmsnorm_weight, L0_ffn_Wg, L0_ffn_Wu, L0_ffn_Wd)
    return x

_drawn_inputs = setup_inputs


def setup_inputs(seed=0):
    import zlib

    import numpy as np

    out = dict(_drawn_inputs(seed))
    spreads = {}
    factors = {}
    for name, (base, spread) in spreads.items():
        noise = np.random.default_rng([zlib.crc32(name.encode()), seed]).standard_normal(out[name].shape)
        drawn = base * np.exp(spread * noise) if base else spread * noise
        out[name] = jnp.asarray(drawn.astype(out[name].dtype))
    for name, factor in factors.items():
        out[name] = (out[name] * factor).astype(out[name].dtype)
    return out
```

```python
import math
from contextlib import ExitStack

import concourse.bass as bass
from concourse import mybir
from concourse.alu_op_type import AluOpType as ALU

F32 = mybir.dt.float32
BF16 = mybir.dt.bfloat16
ACT = mybir.ActivationFunctionType
AX_X = mybir.AxisListType.X

P = 128
HALF = 512
HEADS = HALF // P
MAGIC = 1.5 * 2.0 ** 23
QMAX = 127.0
TAKEN = -3.0e38
LN_EPS = 1e-5
RMS_EPS = 1e-6
STEP_USES = 22
RING = 4

C_FWD = 0
C_FWDU = 4 * P
C_INV = 8 * P
C_AGG = C_INV + 4 * 256
C_SUM = C_AGG + 4 * P
C_IDENT = C_SUM + P
C_END = C_IDENT + P


def dft_constants():
    import numpy as np
    L = 2 * P
    t = np.arange(L, dtype=np.float64)[:, None]
    out = np.zeros((P, C_END), np.float64)
    for eo in range(2):
        f = (2 * np.arange(64) + eo)[None, :]
        re, im = np.cos(2 * np.pi * f * t / L), -np.sin(2 * np.pi * f * t / L)
        plain = np.concatenate([re, im], axis=1)
        swapped = np.concatenate([im, re], axis=1)
        if eo == 0:
            plain[:, 64] = np.cos(np.pi * t[:, 0])
            swapped[:, 0] = 0.0
            swapped[:, 64] = 0.0
        for kind, m in enumerate((plain, swapped)):
            j = 2 * kind + eo
            out[:, C_FWD + j * P:C_FWD + (j + 1) * P] = m[:P]
            u = m[:P].copy()
            u[P - 1] += m[P:].sum(axis=0)
            if j == 2:
                u[P - 1, 0] = 1.0
            out[:, C_FWDU + j * P:C_FWDU + (j + 1) * P] = u
        lag = np.arange(L)[None, :]
        c = 2 * np.cos(2 * np.pi * f.T * lag / L) / L
        s = 2 * np.sin(2 * np.pi * f.T * lag / L) / L
        inv_plain = np.concatenate([c, c], axis=0)
        inv_corr = np.concatenate([s, -s], axis=0)
        inv_agg = np.concatenate([-s, s], axis=0)
        if eo == 0:
            inv_plain[0] = 1.0 / L
            inv_plain[64] = np.cos(np.pi * lag[0]) / L
            for m in (inv_corr, inv_agg):
                m[0] = 0.0
                m[64] = 0.0
        for kind, (m, a) in enumerate(((inv_plain, inv_plain), (inv_corr, inv_agg))):
            j = 2 * kind + eo
            out[:, C_INV + j * L:C_INV + (j + 1) * L] = m
            out[:, C_AGG + j * P:C_AGG + (j + 1) * P] = a[:, :P]
    out[0, C_SUM:C_SUM + P] = 1.0
    out[:, C_IDENT:C_END] = np.eye(P)
    return out.astype(np.float32)


def row_tiles(I, B):
    per = I // B
    return per, [(o, min(P, per - o)) for o in range(0, per, P)]


def attention_and_weights(nc, sems, io, scratch):
    B, L, D = io["x"].shape
    I = io["wg"].shape[0]
    UNITS = 2 * B
    TOPK = int(2 * math.log(L))
    PER, ROWS = row_tiles(I, B)
    NK = D // P
    NI = -(-I // P)
    WD_HALF = NI // 2
    WD_GROUPS = [(0, 4), (4, 8), (8, 11)]
    assert L == 2 * P and D == 2 * HALF and len(ROWS) == 3 and NI == 22 and 8 < TOPK < 16

    ctx = ExitStack()
    with ctx:
        def sb(name, shape, dt=F32):
            return ctx.enter_context(nc.sbuf_tensor(name, shape, dt))

        def sem(name):
            return sems.enter_context(nc.semaphore(name))

        const = sb("const", [P, C_END])
        identb = sb("identb", [P, P], BF16)
        xl = sb("xl", [P, 2, D])
        xr = [sb(f"xr{h}", [P, 2, HALF]) for h in range(2)]
        ck = [sb(f"ck{h}", [P, 2, HALF]) for h in range(2)]
        bn = sb("bn", [P, 2, 2, 6])
        mv = sb("mv", [P, 2, 2])
        veps = sb("veps", [P, 2])
        minus_half = sb("minus_half", [P, 2])
        rstd = sb("rstd", [P, 2])
        nmr = sb("nmr", [P, 2])
        qn = sb("qn", [P, 2, HALF])
        qf = sb("qf", [P, 2, HALF])
        kf = sb("kf", [P, 2, HALF])
        QS = sb("QS", [P, 2, HALF])
        KS = [sb(f"KS{h}", [P, 2, 2, HALF]) for h in range(2)]
        US = [sb(f"US{h}", [P, 2, 2, HALF]) for h in range(2)]
        PT = sb("PT", [P, 2, 2, HALF])
        CR = sb("CR", [P, HEADS, L])
        M1 = sb("M1", [P, HEADS, 8])
        M2 = sb("M2", [P, HEADS, 8])
        nmax = sb("nmax", [P, HEADS])
        Z = sb("Z", [P, HEADS])
        rz = sb("rz", [P, HEADS])
        R = sb("R", [P, HEADS, L])
        W = sb("W", [P, HEADS, L])
        dg = sb("dg", [P, HEADS, P])
        WT = sb("WT", [P, 2, HALF])
        WS = sb("WS", [P, 2, 2, HALF])
        S0 = sb("S0", [P, 2, 2, HALF])
        S1 = sb("S1", [P, 2, 2, HALF])
        T0 = sb("T0", [P, 2, 2, HALF])
        gx = sb("gx", [P, 1])
        gt = sb("gt", [P, 1])
        magic = sb("magic", [P, 1])
        wrow = [sb(f"wrow{k}", [P, D]) for k in range(3)]
        wq = [sb(f"wq{k}", [P, D], BF16) for k in range(3)]
        wd = sb("wd", [P, I])
        wdq = sb("wdq", [P, NI * P], BF16)
        am = sb("am", [P, 4])
        ws = [sb(f"ws{h}", [P, 4]) for h in range(2)]
        rw = sb("rw", [P, 4])
        stage = sb("stage", [P, NK, PER], BF16)
        stage_d = sb("stage_d", [P, WD_HALF, P], BF16)

        bank = [ctx.enter_context(nc.psum_tensor(f"bank{i}", [P, 512], F32)) for i in range(RING)]
        corr = ctx.enter_context(nc.psum_tensor("corr", [P, HEADS, L], F32))
        agg = [ctx.enter_context(nc.psum_tensor(f"agg{i}", [P, HALF], F32)) for i in range(2)]

        held = sem("held")
        const_in = sem("const_in")
        gx_in = sem("gx_in")
        x_in = sem("x_in")
        xr_in = [sem(f"xr_in{h}") for h in range(2)]
        ctx_in = [sem(f"ctx_in{h}") for h in range(2)]
        w_in = [sem(f"w_in{k}") for k in range(3)]
        wd_in = sem("wd_in")
        x1_out = [sem(f"x1_out{h}") for h in range(2)]
        stage_out = sem("stage_out")
        stage_d_out = sem("stage_d_out")
        ws_out = [sem(f"ws_out{h}") for h in range(2)]
        set_up = sem("set_up")
        ident_done = sem("ident_done")
        gate_done = sem("gate_done")
        bn_done = sem("bn_done")
        mv_done = sem("mv_done")
        veps_done = sem("veps_done")
        rstd_done = sem("rstd_done")
        ln_done = sem("ln_done")
        qn_done = sem("qn_done")
        fold_done = sem("fold_done")
        u_done = sem("u_done")
        ring_full = sem("ring_full")
        ring_free = sem("ring_free")
        prod_done = sem("prod_done")
        corr_done = sem("corr_done")
        cr_done = sem("cr_done")
        top8_done = sem("top8_done")
        nmax_done = sem("nmax_done")
        rep8_done = sem("rep8_done")
        top16_done = sem("top16_done")
        pad_done = sem("pad_done")
        rep16_done = sem("rep16_done")
        exp_done = sem("exp_done")
        mask_done = sem("mask_done")
        rz_done = sem("rz_done")
        dg_done = sem("dg_done")
        aggp_done = sem("aggp_done")
        add_done = sem("add_done")
        agg_done = sem("agg_done")
        x1_done = sem("x1_done")
        am_done = sem("am_done")
        ws_done = sem("ws_done")
        rw_done = sem("rw_done")
        y_done = sem("y_done")
        yd_done = sem("yd_done")
        wq_done = sem("wq_done")
        wdq_done = sem("wdq_done")

        ident = const[:, C_IDENT:C_END]

        def fwd(j):
            return const[:, C_FWD + j * P:C_FWD + (j + 1) * P]

        def fwdu(j):
            return const[:, C_FWDU + j * P:C_FWDU + (j + 1) * P]

        def inv(j):
            return const[:, C_INV + j * L:C_INV + (j + 1) * L]

        def agg_inv(j):
            return const[:, C_AGG + j * P:C_AGG + (j + 1) * P]

        class Step:

            def __init__(self, s, h, batch, front=True, back=True):
                self.s, self.h, self.batch, self.front, self.back = s, h, batch, front, back
                self.first_use = s * STEP_USES - 6 if back else 0
                self.first_bank = 2 if back and h == 0 else 0
                self.at = {"fwd": 0, "wt": 10 if front else 0, "wfwd": 12 if front else 2,
                           "tw": 16 if back else 10}
                self.back_batch = batch if h == 1 else batch - 1
                self.static = isinstance(s, int)

            def use(self, kind, i):
                n = self.at[kind] + i
                return self.first_use + n, bank[(self.first_bank + n) % RING]

            def more_fronts(self):
                return not (self.static and self.s >= UNITS - 1)

        def steps(eng):
            yield Step(0, 0, 0, back=False)
            yield Step(1, 1, 0)
            yield Step(2, 0, 1)
            with eng.Fori(1, B - 1) as b:
                yield Step(2 * b + 1, 1, b)
                yield Step(2 * b + 2, 0, b + 1)
            yield Step(UNITS - 1, 1, B - 1)
            yield Step(UNITS, 0, B, front=False)

        x_d = io["x"].rearrange("b (t p) d -> b p t d", p=P)
        c_d = io["ctx"].rearrange("b (t p) d -> b p t d", p=P)
        x1_d = scratch["x1"].rearrange("b (t p) d -> b p t d", p=P)
        wgu_d = [io[n].rearrange("(b r) d -> b r d", r=PER) for n in ("wg", "wu")]
        wd_d = io["wd"].rearrange("(b p) i -> b p i", p=P)
        ws_gu_d = [scratch[n].rearrange("(b r) -> b r", r=PER) for n in ("ws_g", "ws_u")]
        ws_d_d = scratch["ws_d"].rearrange("(b p o) -> b p o", p=P, o=1)
        wT_gu_d = [scratch[n].rearrange("p k (b r) -> b p k r", r=PER) for n in ("wT_g", "wT_u")]
        wT_d_d = scratch["wT_d"].rearrange("p n (b d) -> b p n d", d=P)

        block = ctx.enter_context(nc.Block())

        @block.sync
        def _(sp):
            def load_weights(h, batch):
                for k, (o, n) in enumerate(ROWS):
                    sp.dma_start(wrow[k][0:n, :], wgu_d[h][batch, o:o + n, :]).then_inc(w_in[k], 16)
                if h == 0:
                    sp.dma_start(wd[:, :], wd_d[batch]).then_inc(wd_in, 16)

            def load_ctx(h, batch):
                sp.dma_start(ck[h][:, :, :], c_d[batch, :, :, h * HALF:(h + 1) * HALF]).then_inc(ctx_in[h], 16)

            sp.dma_start(xl[:, :, :], x_d[0]).then_inc(x_in, 16)
            load_ctx(0, 0)
            sp.dma_start(const[:, :], io["const"]).then_inc(const_in, 16)
            load_weights(0, 0)
            sp.dma_start(gx[:, :], io["g_x"].partition_broadcast(P)).then_inc(gx_in, 16)
            for q in steps(sp):
                s, h, batch = q.s, q.h, q.batch
                if q.front:
                    if q.more_fronts():
                        sp.wait_ge(u_done, s)
                        sp.sem_inc(held, 1)
                        if h == 0:
                            load_ctx(1, batch)
                        else:
                            load_ctx(0, batch + 1)
                            sp.wait_ge(qn_done, 2 * (s + 1))
                            sp.sem_inc(held, 1)
                            sp.dma_start(xl[:, :, :], x_d[batch + 1]).then_inc(x_in, 16)
                    sp.wait_ge(x1_out[h], 16 * batch)
                    sp.sem_inc(held, 1)
                    sp.dma_start(xr[h][:, :, :], x_d[batch, :, :, h * HALF:(h + 1) * HALF]).then_inc(xr_in[h], 16)
                    sp.wait_ge(ws_done, s + 1)
                    sp.sem_inc(held, 1)
                    for k, (o, n) in enumerate(ROWS):
                        sp.dma_start(ws_gu_d[h][batch, o:o + n].rearrange("(p o) -> p o", o=1),
                                     ws[h][0:n, k:k + 1]).then_inc(ws_out[h], 16)
                    if h == 0:
                        sp.dma_start(ws_d_d[batch], ws[h][:, 3:4]).then_inc(ws_out[h], 16)
                    if q.more_fronts():
                        sp.wait_ge(wq_done, 3 * (s + 1))
                        sp.sem_inc(held, 1)
                        if h == 1:
                            sp.wait_ge(wdq_done, batch + 1)
                            sp.sem_inc(held, 1)
                        load_weights(1 - h, batch if h == 0 else batch + 1)
                if q.back:
                    sp.wait_ge(x1_done, 2 * s)
                    sp.sem_inc(held, 1)
                    hb = 1 - h
                    sp.dma_start(x1_d[q.back_batch, :, :, hb * HALF:(hb + 1) * HALF],
                                 xr[hb][:, :, :]).then_inc(x1_out[hb], 16)
                if q.front:
                    sp.wait_ge(ring_free, q.use("tw", 5)[0] + 1)
                    sp.sem_inc(held, 1)
                    sp.dma_start(wT_gu_d[h][batch], stage[:, :, :]).then_inc(stage_out, 16)
                    sp.dma_start(wT_d_d[batch, :, h * WD_HALF:(h + 1) * WD_HALF, :],
                                 stage_d[:, :, :]).then_inc(stage_d_out, 16)
            for h in range(2):
                sp.wait_ge(x1_out[h], 16 * B)
                sp.wait_ge(ws_out[h], (64 - 16 * h) * B)
            sp.wait_ge(stage_out, 16 * UNITS)
            sp.wait_ge(stage_d_out, 16 * UNITS)

        @block.gpsimd
        def _(pool):
            def row_rstd(batch):
                pool.wait_ge(veps_done, batch + 1)
                pool.tensor_tensor(rstd[:, :], veps[:, :], minus_half[:, :], ALU.pow).then_inc(rstd_done, 1)

            def fold(s, h, batch):
                pool.wait_ge(ctx_in[h], 16 * (batch + 1))
                pool.wait_ge(u_done, s)
                pool.tensor_tensor(kf[:, 0, :], ck[h][:, 0, :], ck[h][:, 1, :], ALU.add).then_inc(fold_done, 1)
                pool.tensor_tensor(kf[:, 1, :], ck[h][:, 0, :], ck[h][:, 1, :], ALU.subtract).then_inc(fold_done, 1)
                pool.wait_ge(qn_done, 2 * (s + 1))
                pool.tensor_tensor(qf[:, 0, :], qn[:, 0, :], qn[:, 1, :], ALU.add).then_inc(fold_done, 1)
                pool.tensor_tensor(qf[:, 1, :], qn[:, 0, :], qn[:, 1, :], ALU.subtract).then_inc(fold_done, 1)

            pool.memset(minus_half[:, :], -0.5).then_inc(set_up, 1)
            pool.memset(magic[:, :], MAGIC).then_inc(set_up, 1)
            pool.memset(am[:, :], 0.0).then_inc(set_up, 1)
            pool.memset(wdq[:, I:NI * P], 0.0).then_inc(set_up, 1)
            pool.wait_ge(set_up, 4)
            row_rstd(0)
            fold(0, 0, 0)
            for q in steps(pool):
                s, h, batch = q.s, q.h, q.batch
                if h == 1 and q.more_fronts():
                    row_rstd(batch + 1)
                if q.back:
                    for k in range(2):
                        pool.wait_ge(aggp_done, 6 * (s - 1) + k + 3)
                        pool.tensor_tensor(S0[:, k], S0[:, k], S1[:, k], ALU.add).then_inc(add_done, 1)
                if q.front and q.more_fronts():
                    fold(s + 1, 1 - h, batch if h == 0 else batch + 1)

        @block.scalar
        def _(act):
            def normalise(s, h, batch):
                act.wait_ge(ln_done, batch + 1)
                act.wait_ge(fold_done, 4 * s)
                for t in range(2):
                    act.activation(qn[:, t, :], xl[:, t, h * HALF:(h + 1) * HALF], ACT.Identity,
                                   bias=nmr[:, t:t + 1], scale=rstd[:, t:t + 1]).then_inc(qn_done, 1)

            def empty(q, kind, i, out, src=None):
                n, b = q.use(kind, i)
                act.wait_ge(ring_full, n + 1)
                act.activation(out, b[:, :] if src is None else src(b), ACT.Copy).then_inc(ring_free, 1)

            def empty_weights(q, g):
                if g == 0:
                    act.wait_ge(stage_out, 16 * q.s)
                    act.wait_ge(stage_d_out, 16 * q.s)
                if g < 3:
                    o, n = ROWS[g]
                    empty(q, "tw", g, stage[:, :, o:o + n],
                          lambda b: b[:, :].bitcast(BF16).rearrange("p (k r) -> p k r", r=P)[:, :, 0:n])
                else:
                    a, e = WD_GROUPS[g - 3]
                    empty(q, "tw", g, stage_d[:, a:e, :],
                          lambda b: b[:, :].bitcast(BF16)[:, 0:(e - a) * P].rearrange("p (k r) -> p k r", r=P))

            act.wait_ge(const_in, 16)
            act.activation(identb[:, :], ident, ACT.Copy).then_inc(ident_done, 1)
            act.wait_ge(gx_in, 16)
            act.activation(gt[:, :], gx[:, :], ACT.Tanh).then_inc(gate_done, 1)
            act.wait_ge(set_up, 4)
            normalise(0, 0, 0)
            for q in steps(act):
                s, h, batch = q.s, q.h, q.batch
                if q.front:
                    act.wait_ge(prod_done, 2 * s)
                    for i in range(2):
                        empty(q, "fwd", i, QS[:, i, :])
                    if q.back:
                        act.wait_ge(aggp_done, 6 * (s - 1))
                    for i in range(4):
                        empty(q, "fwd", 2 + i, KS[h][:, i // 2, i % 2, :])
                    for i in range(4):
                        empty(q, "fwd", 6 + i, US[h][:, i // 2, i % 2, :])
                if q.back:
                    for i in range(2):
                        empty(q, "wt", i, WT[:, i, :])
                    act.wait_ge(aggp_done, 6 * (s - 1))
                    for i in range(4):
                        empty(q, "wfwd", i, WS[:, i // 2, i % 2, :])
                if q.front:
                    act.wait_ge(rw_done, s + 1)
                    for k, (o, n) in enumerate(ROWS):
                        act.activation(wrow[k][0:n, :], wrow[k][0:n, :], ACT.Identity,
                                       bias=magic[0:n, :], scale=rw[0:n, k:k + 1]).then_inc(y_done, 1)
                    if h == 0:
                        act.activation(wd[:, :], wd[:, :], ACT.Identity,
                                       bias=magic[:, :], scale=rw[:, 3:4]).then_inc(yd_done, 1)
                    if q.more_fronts():
                        normalise(s + 1, 1 - h, batch if h == 0 else batch + 1)
                    act.wait_ge(rep8_done, HEADS * s)
                    for n in range(2):
                        act.wait_ge(corr_done, 2 * s + n + 1)
                        act.activation(CR[:, 2 * n:2 * n + 2, :], corr[:, 2 * n:2 * n + 2, :], ACT.Copy).then_inc(cr_done, 1)
                    empty_weights(q, 0)
                    act.wait_ge(nmax_done, s + 1)
                    for n in range(HEADS):
                        act.activation(W[:, n, :], CR[:, n, :], ACT.Exp,
                                       bias=nmax[:, n:n + 1]).then_inc(exp_done, 1)
                    for g in range(1, 6):
                        empty_weights(q, g)

        @block.vector
        def _(dve):
            def row_stats(batch):
                dve.wait_ge(x_in, 16 * (batch + 1))
                for t in range(2):
                    for c in range(2):
                        dve.bn_stats(bn[:, t, c, :], xl[:, t, c * HALF:(c + 1) * HALF]).then_inc(bn_done, 1)
                dve.wait_ge(bn_done, 4 * (batch + 1))
                dve.sem_inc(held, 1)
                for t in range(2):
                    dve.bn_aggr(mv[:, t, :], bn[:, t, :, :]).then_inc(mv_done, 1)
                dve.wait_ge(mv_done, 2 * (batch + 1))
                dve.tensor_scalar(veps[:, :], mv[:, :, 1], LN_EPS, None, ALU.add).then_inc(veps_done, 1)
                dve.wait_ge(rstd_done, batch + 1)
                dve.scalar_tensor_tensor(out=nmr[:, :], in0=mv[:, :, 0], scalar=-1.0, in1=rstd[:, :],
                                         op0=ALU.mult, op1=ALU.mult).then_inc(ln_done, 1)

            row_stats(0)
            dve.wait_ge(set_up, 4)
            dve.wait_ge(const_in, 16)
            for q in steps(dve):
                s, h, batch = q.s, q.h, q.batch
                if q.front:
                    if q.back:
                        dve.wait_ge(corr_done, 2 * s)
                    for k in range(2):
                        dve.wait_ge(ring_free, q.use("fwd", 3 + 2 * k)[0] + 1)
                        dve.tensor_tensor(PT[:, k], QS[:, :, :], KS[h][:, k], ALU.mult).then_inc(prod_done, 1)
                    seen = 7 * batch + (4 if h == 1 else 0)
                    for k, (o, n) in enumerate(ROWS):
                        dve.wait_ge(w_in[k], 16 * (s + 1))
                        dve.tensor_reduce(am[0:n, k:k + 1], wrow[k][0:n, :], AX_X, ALU.max,
                                          apply_absolute_value=True).then_inc(am_done, 1)
                    n = 3
                    if h == 0:
                        n = 4
                        dve.wait_ge(wd_in, 16 * (batch + 1))
                        dve.tensor_reduce(am[:, 3:4], wd[:, :], AX_X, ALU.max,
                                          apply_absolute_value=True).then_inc(am_done, 1)
                    dve.wait_ge(ws_out[h], (64 - 16 * h) * batch)
                    dve.wait_ge(am_done, seen + n)
                    dve.tensor_scalar(ws[h][:, 0:n], am[:, 0:n], 1.0 / QMAX, 1e-8, ALU.mult, ALU.max).then_inc(ws_done, 1)
                    dve.wait_ge(ws_done, s + 1)
                    dve.reciprocal(rw[:, 0:n], ws[h][:, 0:n]).then_inc(rw_done, 1)
                    if h == 1 and q.more_fronts():
                        row_stats(batch + 1)
                if q.back:
                    hb = 1 - h
                    dve.wait_ge(agg_done, 2 * (s - 1))
                    for out, spec, half in ((S0, KS, 0), (S1, US, 1), (T0, US, 0)):
                        if half == 0:
                            dve.wait_ge(ring_free, q.use("wfwd", 1)[0] + 1)
                        else:
                            dve.wait_ge(ring_free, q.use("wfwd", 3)[0] + 1)
                        for k in range(2):
                            dve.tensor_tensor(out[:, k], spec[hb][:, k], WS[:, half], ALU.mult).then_inc(aggp_done, 1)
                if q.front:
                    dve.wait_ge(y_done, 3 * (s + 1))
                    for k, (o, n) in enumerate(ROWS):
                        dve.tensor_scalar(wq[k][0:n, :], wrow[k][0:n, :], MAGIC, None, ALU.subtract).then_inc(wq_done, 1)
                    if h == 0:
                        dve.wait_ge(yd_done, batch + 1)
                        dve.tensor_scalar(wdq[:, 0:I], wd[:, :], MAGIC, None, ALU.subtract).then_inc(wdq_done, 1)
                    for n in range(HEADS):
                        if n % 2 == 0:
                            dve.wait_ge(cr_done, 2 * s + n // 2 + 1)
                            dve.sem_inc(held, 1)
                        dve.max(M1[:, n, :], CR[:, n, :]).then_inc(top8_done, 1)
                    dve.wait_ge(top8_done, HEADS * (s + 1))
                    dve.tensor_scalar(nmax[:, :], M1[:, :, 0], -1.0, None, ALU.mult).then_inc(nmax_done, 1)
                    for n in range(HEADS):
                        dve.match_replace(R[:, n, :], M1[:, n, :], CR[:, n, :], TAKEN).then_inc(rep8_done, 1)
                    dve.wait_ge(rep8_done, HEADS * (s + 1))
                    dve.sem_inc(held, 1)
                    for n in range(HEADS):
                        dve.max(M2[:, n, :], R[:, n, :]).then_inc(top16_done, 1)
                    dve.wait_ge(top16_done, HEADS * (s + 1))
                    dve.memset(M2[:, :, TOPK - 8:8], TAKEN).then_inc(pad_done, 1)
                    dve.wait_ge(pad_done, s + 1)
                    dve.sem_inc(held, 1)
                    for n in range(HEADS):
                        dve.match_replace(R[:, n, :], M2[:, n, :], R[:, n, :], TAKEN).then_inc(rep16_done, 1)
                    for n in range(HEADS):
                        dve.wait_ge(rep16_done, HEADS * s + n + 1)
                        dve.wait_ge(exp_done, HEADS * s + n + 1)
                        dve.scalar_tensor_tensor(out=W[:, n, :], in0=R[:, n, :], scalar=-1.0e38, in1=W[:, n, :],
                                                 op0=ALU.is_lt, op1=ALU.mult,
                                                 accum_out=Z[:, n:n + 1]).then_inc(mask_done, 1)
                    dve.wait_ge(mask_done, HEADS * (s + 1))
                    dve.reciprocal(rz[:, :], Z[:, :]).then_inc(rz_done, 1)
                    dve.wait_ge(rz_done, s + 1)
                    for n in range(HEADS):
                        dve.tensor_scalar(dg[:, n, :], ident, rz[:, n:n + 1], None, ALU.mult).then_inc(dg_done, 1)
                if q.back:
                    dve.wait_ge(gate_done, 1)
                    dve.wait_ge(xr_in[hb], 16 * (q.back_batch + 1))
                    for t in range(2):
                        dve.wait_ge(agg_done, 2 * (s - 1) + t + 1)
                        dve.scalar_tensor_tensor(out=xr[hb][:, t, :], in0=agg[t][:, :], scalar=gt[:, 0:1],
                                                 in1=xr[hb][:, t, :], op0=ALU.mult, op1=ALU.add).then_inc(x1_done, 1)

        @block.tensor
        def _(pe):
            def ring(q, kind, i):
                n, b = q.use(kind, i)
                if not (isinstance(n, int) and n < RING):
                    pe.wait_ge(ring_free, n + 1 - RING)
                return b

            def transpose_weights(q, g):
                h = q.h
                if g == 0:
                    pe.wait_ge(wq_done, 3 * (q.s + 1))
                    pe.wait_ge(wdq_done, q.batch + 1)
                b = ring(q, "tw", g)[:, :].bitcast(BF16).rearrange("p (k r) -> p k r", r=P)
                if g < 3:
                    n = ROWS[g][1]
                    for k in range(NK):
                        mm = pe.transpose(b[:, k, 0:n], wq[g][0:n, k * P:(k + 1) * P], identb[0:n, 0:n])
                else:
                    a, e = WD_GROUPS[g - 3]
                    for k in range(a, e):
                        c = h * WD_HALF + k
                        mm = pe.transpose(b[:, k - a, :], wdq[:, c * P:(c + 1) * P], identb[:, :])
                mm.then_inc(ring_full, 1)

            pe.wait_ge(set_up, 4)
            pe.wait_ge(ident_done, 1)
            for q in steps(pe):
                s, h, batch = q.s, q.h, q.batch
                if q.front:
                    pe.wait_ge(fold_done, 4 * (s + 1))
                    for i in range(6):
                        eo = i % 2
                        src = qf if i < 2 else kf
                        pe.matmul(ring(q, "fwd", i)[:, :], fwd((0, 1, 0, 1, 2, 3)[i]), src[:, eo, :],
                                  start=True, stop=True).then_inc(ring_full, 1)
                    for i in range(4):
                        pe.matmul(ring(q, "fwd", 6 + i)[:, :], fwdu(i), ck[h][:, 1, :],
                                  start=True, stop=True).then_inc(ring_full, 1)
                    pe.wait_ge(ring_full, q.use("fwd", 9)[0] + 1)
                    pe.nop().then_inc(u_done, 1)
                if q.back:
                    pe.wait_ge(dg_done, HEADS * s)
                    for half in range(2):
                        b = ring(q, "wt", half)
                        for n in range(HEADS):
                            mm = pe.matmul(b[:, n * P:(n + 1) * P], W[:, n, half * P:(half + 1) * P], dg[:, n, :],
                                           start=True, stop=True)
                        mm.then_inc(ring_full, 1)
                    for i in range(4):
                        if i % 2 == 0:
                            pe.wait_ge(ring_free, q.use("wt", i // 2)[0] + 1)
                        pe.matmul(ring(q, "wfwd", i)[:, :], fwd(i % 2), WT[:, i // 2, :],
                                  start=True, stop=True).then_inc(ring_full, 1)
                if q.front:
                    pe.wait_ge(prod_done, 2 * (s + 1))
                    pe.wait_ge(cr_done, 2 * s)
                    for n in range(HEADS):
                        for j in range(4):
                            mm = pe.matmul(corr[:, n, :], PT[:, j // 2, j % 2, n * P:(n + 1) * P], inv(j),
                                           start=(j == 0), stop=(j == 3))
                        if n % 2 == 1:
                            mm.then_inc(corr_done, 1)
                    transpose_weights(q, 0)
                if q.back:
                    pe.wait_ge(add_done, 2 * s)
                    pe.wait_ge(x1_done, 2 * (s - 1))
                    for j in range(4):
                        mm = pe.matmul(agg[0][:, :], agg_inv(j), S0[:, j // 2, j % 2, :], start=(j == 0), stop=(j == 3))
                    mm.then_inc(agg_done, 1)
                if q.front:
                    transpose_weights(q, 1)
                if q.back:
                    pe.wait_ge(aggp_done, 6 * s)
                    for j in range(4):
                        pe.matmul(agg[1][:, :], agg_inv(j), T0[:, j // 2, j % 2, :], start=(j == 0), stop=False)
                    pe.matmul(agg[1][:, :], const[:, C_SUM:C_SUM + P], S0[:, 1, 0, :],
                              start=False, stop=True).then_inc(agg_done, 1)
                if q.front:
                    for g in range(2, 6):
                        transpose_weights(q, g)


def feed_forward(nc, sems, io, scratch, out):
    B, L, D = io["x"].shape
    I = io["wg"].shape[0]
    NK = D // P
    NI = -(-I // P)
    LAST = I - (NI - 1) * P
    PER, _ = row_tiles(I, B)

    ctx = ExitStack()
    with ctx:
        def sb(name, shape, dt=F32):
            return ctx.enter_context(nc.sbuf_tensor(name, shape, dt))

        def sem(name):
            return sems.enter_context(nc.semaphore("f_" + name))

        wgT = sb("wgT", [P, NK, I], BF16)
        wuT = sb("wuT", [P, NK, I], BF16)
        wdT = sb("wdT", [P, NI, D], BF16)
        hid = [sb(f"hid{i}", [P, NI, L]) for i in range(2)]
        xin = sb("xin", [P, D])
        qrow = sb("qrow", [P, 2, D], BF16)
        qT = sb("qT", [P, NK, L], BF16)
        res = sb("res", [P, D])
        wn = sb("wn", [P, D])
        wsd = sb("wsd", [P, D])
        gs = [sb(f"gs{i}", [P, L]) for i in range(2)]
        mx = sb("mx", [P, L])
        rb = sb("rb", [P, L])
        sbc = [sb(f"sbc{i}", [P, L]) for i in range(2)]
        identf = sb("identf", [P, P])
        identb = sb("identb2", [P, P], BF16)
        ones = sb("ones", [P, P])
        dg = sb("dg2", [P, 2, P])
        wsg = sb("wsg", [P, NI])
        wsu = sb("wsu", [P, NI])
        small = sb("small", [P, 64])
        gf = small[:, 0:1]
        gt = small[:, 1:2]
        magic = small[:, 2:3]
        minus_half = small[:, 3:4]
        bn = small[:, 4:16].rearrange("p (c k) -> p c k", c=2)
        mv = small[:, 16:18]
        veps = small[:, 18:19]
        rstd = small[:, 19:20]
        ms = small[:, 20:21]
        ms2 = small[:, 21:22]
        r2 = small[:, 22:23]
        a_ = small[:, 23:24]
        amx = small[:, 24:25]
        rs = small[:, 25:26]
        sc = small[:, 26:27]
        smax = small[:, 28:29]
        hm = small[:, 30:32]
        s2 = small[:, 32:34]
        rs2 = small[:, 34:36]
        rr = small[:, 36:38]
        s2raw = small[:, 38:40]
        scol = [small[:, 40 + 2 * i:42 + 2 * i] for i in range(2)]
        s2g = [small[:, 44 + 2 * i:46 + 2 * i] for i in range(2)]

        bank = [ctx.enter_context(nc.psum_tensor(f"gu{i}", [P, 2, L], F32)) for i in range(RING)]
        down = [ctx.enter_context(nc.psum_tensor(f"down{i}", [P, HALF], F32)) for i in range(3)]
        misc = ctx.enter_context(nc.psum_tensor("misc", [P, 512], F32))
        DOWN_BANK = (0, 1, 2, 1)

        held = sem("held")
        const_in = sem("const_in")
        scale_in = sem("scale_in")
        gu_in = [sem(f"gu_in{c}") for c in range(B)]
        wd_in = sem("wd_in")
        x_in = sem("x_in")
        res_in = sem("res_in")
        y_out = sem("y_out")
        set_up = sem("set_up")
        ident_done = sem("ident_done")
        gate_done = sem("gate_done")
        prep = {n: sem("p_" + n) for n in ("bn", "mv", "veps", "rstd", "ms", "ms2", "r2", "a", "u", "amx", "smax", "s",
                                           "rs", "sc", "y", "q")}
        dgs_done = sem("dgs_done")
        misc_full = sem("misc_full")
        misc_free = sem("misc_free")
        gu_full = sem("gu_full")
        gs_done = sem("gs_done")
        si_done = sem("si_done")
        hid_done = sem("hid_done")
        abs_done = sem("abs_done")
        mx_done = sem("mx_done")
        scaled_done = sem("scaled_done")
        magic_done = sem("magic_done")
        q2_done = sem("q2_done")
        s2raw_done = sem("s2raw_done")
        s2_done = sem("s2_done")
        rs2_done = sem("rs2_done")
        rr_done = sem("rr_done")
        s2g_done = sem("s2g_done")
        dgr_done = sem("dgr_done")
        down_full = sem("down_full")
        down_scaled = sem("down_scaled")
        y_done = sem("y_done")

        x1_d = scratch["x1"].rearrange("b (t p) d -> b t p d", p=P)
        out_d = out.rearrange("b (t p) d -> b t p d", p=P)

        def rows(i):
            return P if i < NI - 1 else LAST

        def q2(par, i):
            return hid[par][:, i, :].bitcast(BF16).rearrange("p (t k) -> p t k", t=2)[:, :, 0:P]

        class Step:
            def __init__(self, b, par, hidden=True, down=True, more=True):
                self.b, self.par, self.hidden, self.down, self.more = b, par, hidden, down, more
                self.first_bank = 2 * par

            def use(self, i):
                return NI * self.b + i, bank[(self.first_bank + i) % RING]

        def steps(eng):
            yield Step(0, 0, down=False)
            yield Step(1, 1)
            yield Step(2, 0)
            with eng.Fori(1, (B - 2) // 2) as k:
                yield Step(2 * k + 1, 1)
                yield Step(2 * k + 2, 0)
            yield Step(B - 1, 1, more=False)
            yield Step(B, 0, hidden=False, more=False)

        def misc_use(b, n):
            if n < 3:
                return n if isinstance(b, int) and b == 0 else 5 * b - 2 + n
            return 5 * b + n if isinstance(b, int) and b == B - 1 else 5 * b + n + 3

        PREP_AT = {3: 0, 11: 1}

        block = ctx.enter_context(nc.Block())

        @block.sync
        def _(sp):
            def load_x(b, t):
                if not (isinstance(b, int) and b == 0 and t == 0):
                    sp.wait_ge(prep["q"], 2 * b + t)
                    sp.sem_inc(held, 1)
                sp.dma_start(xin[:, :], x1_d[b, t]).then_inc(x_in, 16)

            load_x(0, 0)
            sp.dma_start(wn[:, :], io["w_rms"].partition_broadcast(P)).then_inc(const_in, 16)
            sp.dma_start(identf[:, :], io["const"][:, C_IDENT:C_END]).then_inc(const_in, 16)
            sp.dma_start(gf, io["g_f"].partition_broadcast(P)).then_inc(const_in, 16)
            for tile, src in ((wsg, scratch["ws_g"]), (wsu, scratch["ws_u"])):
                full = (NI - 1) * P
                sp.dma_start(tile[:, 0:NI - 1], src[0:full].rearrange("(n p) -> p n", p=P),
                             allow_slow_non_contiguous=True).then_inc(scale_in, 16)
                sp.dma_start(tile[0:LAST, NI - 1:NI], src[full:I].rearrange("(p o) -> p o", o=1)).then_inc(scale_in, 16)
            for c in range(B):
                for tile, src in ((wgT, scratch["wT_g"]), (wuT, scratch["wT_u"])):
                    sp.dma_start(tile[:, :, c * PER:(c + 1) * PER], src[:, :, c * PER:(c + 1) * PER]).then_inc(gu_in[c], 16)
                if c == 0:
                    load_x(0, 1)
            sp.dma_start(wdT[:, :, :], scratch["wT_d"]).then_inc(wd_in, 16)
            sp.dma_start(wsd[:, :], scratch["ws_d"].partition_broadcast(P)).then_inc(wd_in, 16)
            for q in steps(sp):
                b = q.b
                if q.more:
                    load_x(b + 1, 0)
                    load_x(b + 1, 1)
                if q.down:
                    for t in range(2):
                        if not (isinstance(b, int) and b == 1 and t == 0):
                            sp.wait_ge(y_out, 16 * (2 * (b - 1) + t))
                            sp.sem_inc(held, 1)
                        sp.dma_start(res[:, :], x1_d[b - 1, t]).then_inc(res_in, 16)
                        sp.wait_ge(y_done, 4 * (b - 1) + 2 * t + 2)
                        sp.sem_inc(held, 1)
                        sp.dma_start(out_d[b - 1, t], res[:, :]).then_inc(y_out, 16)
            sp.wait_ge(y_out, 16 * 2 * B)

        @block.gpsimd
        def _(pool):
            pool.memset(minus_half, -0.5).then_inc(set_up, 1)
            pool.memset(magic, MAGIC).then_inc(set_up, 1)
            pool.memset(ones[:, :], 1.0).then_inc(set_up, 1)
            pool.wait_ge(set_up, 3)

            def roots(n):
                pool.wait_ge(prep["veps"], n + 1)
                pool.tensor_tensor(rstd, veps, minus_half, ALU.pow).then_inc(prep["rstd"], 1)
                pool.wait_ge(prep["ms2"], n + 1)
                pool.tensor_tensor(r2, ms2, minus_half, ALU.pow).then_inc(prep["r2"], 1)

            roots(0)
            roots(1)
            for q in steps(pool):
                if q.more:
                    roots(2 * q.b + 2)
                    roots(2 * q.b + 3)

        @block.scalar
        def _(act):
            def round_input(n):
                act.wait_ge(prep["sc"], n + 1)
                act.activation(xin[:, :], xin[:, :], ACT.Identity, bias=magic, scale=sc).then_inc(prep["y"], 1)

            def empty_misc(b, n, out, src):
                act.wait_ge(misc_full, misc_use(b, n) + 1)
                act.activation(out, src, ACT.Copy).then_inc(misc_free, 1)

            def empty_input(b, par):
                for t in range(2):
                    empty_misc(b, t, qT[:, :, t * P:(t + 1) * P],
                               misc[:, :].bitcast(BF16).rearrange("p (k r) -> p k r", r=P))
                empty_misc(b, 2, sbc[par][:, :], misc[:, 0:L])

            def magnitude(q, i):
                n = rows(i)
                use, bk = q.use(i)
                act.wait_ge(hid_done, use + 1)
                act.activation(bk[0:n, 0, :], hid[q.par][0:n, i, :], ACT.Abs).then_inc(abs_done, 1)

            act.wait_ge(const_in, 48)
            act.activation(identb[:, :], identf[:, :], ACT.Copy).then_inc(ident_done, 1)
            act.activation(gt, gf, ACT.Tanh).then_inc(gate_done, 1)
            act.wait_ge(set_up, 3)
            round_input(0)
            round_input(1)
            empty_input(0, 0)
            act.wait_ge(scale_in, 64)
            for q in steps(act):
                b, par = q.b, q.par
                for i in range(NI):
                    n = rows(i)
                    if q.hidden:
                        act.wait_ge(gs_done, NI * b + i + 1)
                        act.activation(gs[i % 2][0:n, :], gs[i % 2][0:n, :], ACT.Silu,
                                       scale=wsg[0:n, i:i + 1]).then_inc(si_done, 1)
                    if q.down:
                        act.wait_ge(scaled_done, NI * (b - 1) + i + 1)
                        t = hid[1 - par][0:n, i, :]
                        act.activation(t, t, ACT.Identity, bias=magic[0:n, :]).then_inc(magic_done, 1)
                    if q.hidden and i > 0:
                        magnitude(q, i - 1)
                    if q.more and i in PREP_AT:
                        round_input(2 * (b + 1) + PREP_AT[i])
                if q.hidden:
                    magnitude(q, NI - 1)
                if q.more:
                    empty_input(b + 1, 1 - par)
                if q.hidden:
                    empty_misc(b, 4, rb[:, :], misc[:, 0:L])

        @block.vector
        def _(dve):
            def link(ins, s, n):
                ins.then_inc(s, 1)
                dve.wait_ge(s, n)

            def prepare(n, t, par):
                dve.wait_ge(x_in, 16 * (n + 1))
                for c in range(2):
                    dve.bn_stats(bn[:, c, :], xin[:, c * HALF:(c + 1) * HALF]).then_inc(prep["bn"], 1)
                dve.wait_ge(prep["bn"], 2 * (n + 1))
                dve.sem_inc(held, 1)
                link(dve.bn_aggr(mv, bn), prep["mv"], n + 1)
                dve.tensor_scalar(veps, mv[:, 1:2], LN_EPS, None, ALU.add).then_inc(prep["veps"], 1)
                link(dve.scalar_tensor_tensor(out=xin[:, :], in0=xin[:, :], scalar=mv[:, 0:1], in1=wn[:, :],
                                              op0=ALU.subtract, op1=ALU.mult), prep["u"], n + 1)
                dve.tensor_reduce(amx, xin[:, :], AX_X, ALU.max, apply_absolute_value=True).then_inc(prep["amx"], 1)
                dve.wait_ge(prep["rstd"], n + 1)
                link(dve.scalar_tensor_tensor(out=ms, in0=mv[:, 1:2], scalar=rstd, in1=rstd,
                                              op0=ALU.mult, op1=ALU.mult), prep["ms"], n + 1)
                dve.tensor_scalar(ms2, ms, RMS_EPS, None, ALU.add).then_inc(prep["ms2"], 1)
                dve.wait_ge(prep["r2"], n + 1)
                link(dve.tensor_tensor(a_, rstd, r2, ALU.mult), prep["a"], n + 1)
                dve.wait_ge(prep["amx"], n + 1)
                link(dve.tensor_tensor(smax, amx, a_, ALU.mult), prep["smax"], n + 1)
                s = scol[par][:, t:t + 1]
                link(dve.tensor_scalar(s, smax, 1.0 / QMAX, 1e-8, ALU.mult, ALU.max), prep["s"], n + 1)
                link(dve.reciprocal(rs, s), prep["rs"], n + 1)
                dve.tensor_tensor(sc, a_, rs, ALU.mult).then_inc(prep["sc"], 1)
                dve.tensor_scalar(dg[:, t, :], identf[:, :], s, None, ALU.mult).then_inc(dgs_done, 1)

            def round_input(n, t):
                dve.wait_ge(prep["y"], n + 1)
                dve.tensor_scalar(qrow[:, t, :], xin[:, :], MAGIC, None, ALU.subtract).then_inc(prep["q"], 1)

            def hidden(q, i):
                b, par, n = q.b, q.par, rows(i)
                use, bk = q.use(i)
                dve.wait_ge(si_done, use + 1)
                t = hid[par][0:n, i, :]
                dve.scalar_tensor_tensor(out=t, in0=bk[0:n, 1, :], scalar=wsu[0:n, i:i + 1], in1=gs[i % 2][0:n, :],
                                         op0=ALU.mult, op1=ALU.mult).then_inc(hid_done, 1)

            def running_max(q, i):
                n = rows(i)
                use, bk = q.use(i)
                dve.wait_ge(abs_done, use + 1)
                if i == 0:
                    dve.tensor_copy(mx[:, :], bk[:, 0, :]).then_inc(mx_done, 1)
                else:
                    dve.wait_ge(mx_done, use)
                    dve.tensor_tensor(mx[0:n, :], bk[0:n, 0, :], mx[0:n, :], ALU.max).then_inc(mx_done, 1)

            def scale_hidden(b, par, i):
                n = rows(i)
                t = hid[par][0:n, i, :]
                dve.tensor_tensor(t, t, rb[0:n, :], ALU.mult).then_inc(scaled_done, 1)

            def take_magic_off(b, par, i):
                n = rows(i)
                dve.wait_ge(magic_done, NI * b + i + 1)
                dve.tensor_scalar(q2(par, i)[0:n, :, :], hid[par][0:n, i, :].rearrange("p (t k) -> p t k", t=2), MAGIC, None, ALU.subtract).then_inc(q2_done, 1)

            dve.wait_ge(const_in, 48)
            dve.wait_ge(set_up, 3)
            for t in range(2):
                prepare(t, t, 0)
                round_input(t, t)
            dve.wait_ge(scale_in, 64)
            for q in steps(dve):
                b, par = q.b, q.par
                if q.down:
                    dve.wait_ge(misc_free, misc_use(b - 1, 4) + 1)
                if q.hidden:
                    dve.wait_ge(misc_free, misc_use(b, 2) + 1)
                for i in range(NI + 2):
                    if q.hidden and i < NI:
                        n = rows(i)
                        use, bk = q.use(i)
                        if not (isinstance(b, int) and b == 0 and i < 2):
                            dve.wait_ge(hid_done, use - 1)
                        dve.wait_ge(gu_full, use + 1)
                        dve.tensor_tensor(gs[i % 2][0:n, :], bk[0:n, 0, :], sbc[par][0:n, :], ALU.mult).then_inc(gs_done, 1)
                    if q.down and i < NI:
                        scale_hidden(b - 1, 1 - par, i)
                    if q.hidden and 0 < i <= NI:
                        hidden(q, i - 1)
                    if q.hidden and i > 1:
                        running_max(q, i - 2)
                    if q.down and 0 < i <= NI:
                        take_magic_off(b - 1, 1 - par, i - 1)
                    if q.more and i in PREP_AT:
                        prepare(2 * (b + 1) + PREP_AT[i], PREP_AT[i], 1 - par)
                    if q.more and i - 3 in PREP_AT:
                        round_input(2 * (b + 1) + PREP_AT[i - 3], PREP_AT[i - 3])
                if q.hidden:
                    s = scol[par]
                    dve.wait_ge(misc_full, misc_use(b, 3) + 1)
                    link(dve.tensor_reduce(hm, misc[:, 0:L].rearrange("p (t k) -> p t k", t=2), AX_X, ALU.max),
                         misc_free, misc_use(b, 3) + 1)
                    link(dve.tensor_tensor(s2raw, hm, s, ALU.mult), s2raw_done, b + 1)
                    link(dve.tensor_scalar(s2, s2raw, 1.0 / QMAX, 1e-8, ALU.mult, ALU.max), s2_done, b + 1)
                    link(dve.reciprocal(rs2, s2), rs2_done, b + 1)
                    link(dve.tensor_tensor(rr, rs2, s, ALU.mult), rr_done, b + 1)
                    for t in range(2):
                        dve.tensor_scalar(dg[:, t, :], identf[:, :], rr[:, t:t + 1], None, ALU.mult).then_inc(dgr_done, 1)
                    dve.wait_ge(gate_done, 1)
                    link(dve.tensor_scalar(s2g[par], s2, gt, None, ALU.mult), s2g_done, b + 1)
                if q.down:
                    dve.wait_ge(wd_in, 32)
                    for quarter in range(4):
                        t, c = quarter // 2, quarter % 2
                        n = 4 * (b - 1) + quarter
                        bk = down[DOWN_BANK[quarter]]
                        cols = slice(c * HALF, (c + 1) * HALF)
                        dve.wait_ge(down_full, n + 1)
                        link(dve.scalar_tensor_tensor(out=bk[:, :], in0=bk[:, :], scalar=s2g[1 - par][:, t:t + 1],
                                                      in1=wsd[:, cols], op0=ALU.mult, op1=ALU.mult), down_scaled, n + 1)
                        if c == 0:
                            dve.wait_ge(res_in, 16 * (2 * (b - 1) + t + 1))
                        dve.tensor_tensor(res[:, cols], bk[:, :], res[:, cols], ALU.add).then_inc(y_done, 1)

        @block.tensor
        def _(pe):
            def misc_wait(b, n):
                u = misc_use(b, n)
                if not (isinstance(u, int) and u == 0):
                    pe.wait_ge(misc_free, u)

            def input_transposed(b):
                for t in range(2):
                    pe.wait_ge(prep["q"], 2 * b + t + 1)
                    misc_wait(b, t)
                    for k in range(NK):
                        mm = pe.transpose(misc[:, :].bitcast(BF16)[:, k * P:(k + 1) * P],
                                          qrow[:, t, k * P:(k + 1) * P], identb[:, :])
                    mm.then_inc(misc_full, 1)
                pe.wait_ge(dgs_done, 2 * (b + 1))
                misc_wait(b, 2)
                pe.matmul(misc[:, 0:L], ones[:, :], dg[:, :, :], start=True, stop=True).then_inc(misc_full, 1)

            def down_project(b, quarter, par):
                t, c = quarter // 2, quarter % 2
                pe.wait_ge(y_done, 4 * b if quarter < 3 else 4 * b + 2)
                bk = down[DOWN_BANK[quarter]]
                for i in range(NI):
                    if quarter == 0:
                        pe.wait_ge(q2_done, NI * b + i + 1)
                    n = rows(i)
                    mm = pe.matmul(bk[:, :], q2(par, i)[0:n, t, :],
                                   wdT[0:n, i, c * HALF:(c + 1) * HALF], start=(i == 0), stop=(i == NI - 1))
                mm.then_inc(down_full, 1)

            pe.wait_ge(const_in, 48)
            pe.wait_ge(set_up, 3)
            pe.wait_ge(ident_done, 1)
            input_transposed(0)
            for q in steps(pe):
                b, par = q.b, q.par
                if q.hidden:
                    pe.wait_ge(misc_free, misc_use(b, 1) + 1)
                    for i in range(NI):
                        n = rows(i)
                        if isinstance(b, int) and b == 0:
                            pe.wait_ge(gu_in[(i * P + n - 1) // PER], 32)
                        use, bk = q.use(i)
                        if not (isinstance(b, int) and b == 0 and i < RING):
                            pe.wait_ge(mx_done, use + 1 - RING)
                        for j, wT in enumerate((wgT, wuT)):
                            for k in range(NK):
                                mm = pe.matmul(bk[0:n, j, :], wT[:, k, i * P:i * P + n], qT[:, k, :],
                                               start=(k == 0), stop=(k == NK - 1))
                        mm.then_inc(gu_full, 1)
                if q.more:
                    input_transposed(b + 1)
                if q.hidden:
                    pe.wait_ge(mx_done, NI * (b + 1))
                    misc_wait(b, 3)
                    for t in range(2):
                        mm = pe.transpose(misc[:, t * P:(t + 1) * P], mx[:, t * P:(t + 1) * P], identf[:, :])
                    mm.then_inc(misc_full, 1)
                if q.down:
                    pe.wait_ge(wd_in, 32)
                    down_project(b - 1, 0, 1 - par)
                if q.hidden:
                    pe.wait_ge(dgr_done, 2 * (b + 1))
                    misc_wait(b, 4)
                    pe.matmul(misc[:, 0:L], ones[:, :], dg[:, :, :], start=True, stop=True).then_inc(misc_full, 1)
                if q.down:
                    for quarter in range(1, 4):
                        down_project(b - 1, quarter, 1 - par)


def program(nc, io, out):
    B, L, D = io["x"].shape
    I = io["wg"].shape[0]

    def internal(name, shape, dt=F32):
        return nc.dram_tensor(name, shape, dt, kind="Internal").ap()

    scratch = {
        "x1": internal("x1", (B, L, D)),
        "ws_g": internal("ws_g", (I,)), "ws_u": internal("ws_u", (I,)), "ws_d": internal("ws_d", (D,)),
        "wT_g": internal("wT_g", (P, D // P, I), BF16), "wT_u": internal("wT_u", (P, D // P, I), BF16),
        "wT_d": internal("wT_d", (P, -(-I // P), D), BF16),
    }
    with ExitStack() as sems:
        attention_and_weights(nc, sems, io, scratch)
        feed_forward(nc, sems, io, scratch, out)


INPUTS = {"x": "x", "ctx": "ctx_4096", "g_x": "g_xattn", "g_f": "g_ffn", "w_rms": "L0_ffn_rmsnorm_weight",
          "wg": "L0_ffn_Wg", "wu": "L0_ffn_Wu", "wd": "L0_ffn_Wd"}


def kernel(**inputs):
    import numpy as np
    import concourse.bacc as bacc
    from concourse.bass_utils import run_bass_kernel_spmd

    nc = bacc.Bacc("TRN2", target_bir_lowering=False, num_devices=1)
    arrays = {f"in_{k}": np.ascontiguousarray(inputs[name]) for k, name in INPUTS.items()}
    arrays["in_const"] = dft_constants()
    io = {k[3:]: nc.dram_tensor(k, a.shape, mybir.dt.from_np(a.dtype), kind="ExternalInput").ap()
          for k, a in arrays.items()}
    out = nc.dram_tensor("out", inputs["x"].shape, F32, kind="ExternalOutput").ap()
    program(nc, io, out)
    result = run_bass_kernel_spmd(nc, [arrays], core_ids=[0])
    return result.results[0]["out"]
```

```python
import math
from contextlib import ExitStack

import concourse.bass as bass
from concourse import mybir
from concourse.alu_op_type import AluOpType as ALU

F32 = mybir.dt.float32
BF16 = mybir.dt.bfloat16
ACT = mybir.ActivationFunctionType
AX_X = mybir.AxisListType.X

P = 128
HALF = 512
HEADS = HALF // P
MAGIC = 1.5 * 2.0 ** 23
QMAX = 127.0
TAKEN = -3.0e38
LN_EPS = 1e-5
RMS_EPS = 1e-6
STEP_USES = 22
BACK_USES = 12
RING = 4

C_FWD = 0
C_FWDU = 4 * P
C_INV = 8 * P
C_AGG = C_INV + 4 * P
C_SUM = C_AGG + 4 * P
C_IDENT = C_SUM + P
C_END = C_IDENT + P


def dft_constants():
    import numpy as np
    L = 2 * P
    t = np.arange(L, dtype=np.float64)[:, None]
    out = np.zeros((P, C_END), np.float64)
    for eo in range(2):
        f = (2 * np.arange(64) + eo)[None, :]
        re, im = np.cos(2 * np.pi * f * t / L), -np.sin(2 * np.pi * f * t / L)
        plain = np.concatenate([re, im], axis=1)
        swapped = np.concatenate([im, re], axis=1)
        if eo == 0:
            plain[:, 64] = np.cos(np.pi * t[:, 0])
            swapped[:, 0] = 0.0
            swapped[:, 64] = 0.0
        for kind, m in enumerate((plain, swapped)):
            j = 2 * kind + eo
            out[:, C_FWD + j * P:C_FWD + (j + 1) * P] = m[:P]
            u = m[:P].copy()
            u[P - 1] += m[P:].sum(axis=0)
            if j == 2:
                u[P - 1, 0] = 1.0
            out[:, C_FWDU + j * P:C_FWDU + (j + 1) * P] = u
        lag = np.arange(L)[None, :]
        c = 2 * np.cos(2 * np.pi * f.T * lag / L) / L
        s = 2 * np.sin(2 * np.pi * f.T * lag / L) / L
        inv_plain = np.concatenate([c, c], axis=0)
        inv_corr = np.concatenate([s, -s], axis=0)
        inv_agg = np.concatenate([-s, s], axis=0)
        if eo == 0:
            inv_plain[0] = 1.0 / L
            inv_plain[64] = np.cos(np.pi * lag[0]) / L
            for m in (inv_corr, inv_agg):
                m[0] = 0.0
                m[64] = 0.0
        for kind, (m, a) in enumerate(((inv_plain, inv_plain), (inv_corr, inv_agg))):
            j = 2 * kind + eo
            out[:, C_INV + j * P:C_INV + (j + 1) * P] = m[:, :P]
            out[:, C_AGG + j * P:C_AGG + (j + 1) * P] = a[:, :P]
    out[0, C_SUM:C_SUM + P] = 1.0
    out[:, C_IDENT:C_END] = np.eye(P)
    return out.astype(np.float32)


def row_tiles(I, B):
    per = I // B
    return per, [(o, min(P, per - o)) for o in range(0, per, P)]


def attention_and_weights(nc, sems, io, scratch):
    B, L, D = io["x"].shape
    I = io["wg"].shape[0]
    UNITS = 2 * B
    TOPK = int(2 * math.log(L))
    PER, ROWS = row_tiles(I, B)
    NK = D // P
    NI = -(-I // P)
    WD_HALF = NI // 2
    WD_GROUPS = [(0, 4), (4, 8), (8, 11)]
    assert L == 2 * P and D == 2 * HALF and len(ROWS) == 3 and NI == 22 and 8 < TOPK < 16

    ctx = ExitStack()
    with ctx:
        def sb(name, shape, dt=F32):
            return ctx.enter_context(nc.sbuf_tensor(name, shape, dt))

        def sem(name):
            return sems.enter_context(nc.semaphore(name))

        const = sb("const", [P, C_END])
        identb = sb("identb", [P, P], BF16)
        xl = sb("xl", [P, 2, D])
        xr = [sb(f"xr{h}", [P, 2, HALF]) for h in range(2)]
        ck = [sb(f"ck{h}", [P, 2, HALF]) for h in range(2)]
        bn = sb("bn", [P, 2, 2, 6])
        mv = sb("mv", [P, 2, 2])
        veps = sb("veps", [P, 2])
        minus_half = sb("minus_half", [P, 2])
        rstd = sb("rstd", [P, 2])
        nmr = sb("nmr", [P, 2])
        qn = sb("qn", [P, 2, HALF])
        qf = sb("qf", [P, 2, HALF])
        kf = sb("kf", [P, 2, HALF])
        QS = sb("QS", [P, 2, HALF])
        KS = [sb(f"KS{h}", [P, 2, 2, HALF]) for h in range(2)]
        US = [sb(f"US{h}", [P, 2, 2, HALF]) for h in range(2)]
        PT = sb("PT", [P, 2, 2, HALF])
        CR = sb("CR", [P, HEADS, L])
        M1 = sb("M1", [P, HEADS, 8])
        M2 = sb("M2", [P, HEADS, 8])
        nmax = sb("nmax", [P, HEADS])
        ODD = sb("ODD", [P, HEADS, P])
        Z = sb("Z", [P, HEADS])
        rz = sb("rz", [P, HEADS])
        R = sb("R", [P, HEADS, L])
        W = sb("W", [P, HEADS, L])
        WT = sb("WT", [P, 2, HALF])
        WS = sb("WS", [P, 2, 2, HALF])
        S0 = sb("S0", [P, 2, 2, HALF])
        S1 = sb("S1", [P, 2, 2, HALF])
        T0 = sb("T0", [P, 2, 2, HALF])
        gx = sb("gx", [P, 1])
        gt = sb("gt", [P, 1])
        magic = sb("magic", [P, 2])
        wrow = [[sb(f"wrow{h}_{k}", [P, D]) for k in range(3)] for h in range(2)]
        wq = [sb(f"wq{k}", [P, D], BF16) for k in range(3)]
        wd = sb("wd", [P, I])
        wdq = sb("wdq", [P, NI * P], BF16)
        am = sb("am", [P, 4])
        ws = [sb(f"ws{h}", [P, 4]) for h in range(2)]
        rw = [sb(f"rw{h}", [P, 4]) for h in range(2)]
        stage = sb("stage", [P, NK, PER], BF16)
        stage_d = sb("stage_d", [P, WD_HALF, P], BF16)

        bank = [ctx.enter_context(nc.psum_tensor(f"bank{i}", [P, 512], F32)) for i in range(RING)]
        corr = [ctx.enter_context(nc.psum_tensor(f"corr{i}", [P, HEADS, P], F32)) for i in range(2)]
        agg = [ctx.enter_context(nc.psum_tensor(f"agg{i}", [P, HALF], F32)) for i in range(2)]

        held = sem("held")
        const_in = sem("const_in")
        gx_in = sem("gx_in")
        x_in = sem("x_in")
        xr_in = [sem(f"xr_in{h}") for h in range(2)]
        ctx_in = [sem(f"ctx_in{h}") for h in range(2)]
        w_in = [[sem(f"w_in{h}_{k}") for k in range(3)] for h in range(2)]
        wd_in = sem("wd_in")
        x1_out = [sem(f"x1_out{h}") for h in range(2)]
        stage_out = sem("stage_out")
        stage_d_out = sem("stage_d_out")
        ws_out = [sem(f"ws_out{h}") for h in range(2)]
        set_up = sem("set_up")
        ident_done = sem("ident_done")
        gate_done = sem("gate_done")
        bn_done = sem("bn_done")
        mv_done = sem("mv_done")
        veps_done = sem("veps_done")
        rstd_done = sem("rstd_done")
        ln_done = sem("ln_done")
        qn_done = sem("qn_done")
        fold_done = sem("fold_done")
        u_done = sem("u_done")
        ring_full = sem("ring_full")
        ring_free = sem("ring_free")
        prod_done = sem("prod_done")
        corr_done = sem("corr_done")
        odd_done = sem("odd_done")
        cr_done = sem("cr_done")
        top8_done = sem("top8_done")
        nmax_done = sem("nmax_done")
        rep8_done = sem("rep8_done")
        top16_done = sem("top16_done")
        pad_done = sem("pad_done")
        rep16_done = sem("rep16_done")
        exp_done = sem("exp_done")
        mask_done = sem("mask_done")
        rz_done = sem("rz_done")
        norm_done = sem("norm_done")
        aggp_done = sem("aggp_done")
        t0_done = sem("t0_done")
        add_done = sem("add_done")
        agg_done = sem("agg_done")
        x1_done = sem("x1_done")
        am_done = sem("am_done")
        ws_done = sem("ws_done")
        rw_done = sem("rw_done")
        y_done = sem("y_done")
        yd_done = sem("yd_done")
        wq_done = sem("wq_done")
        wdq_done = sem("wdq_done")

        ident = const[:, C_IDENT:C_END]

        def fwd(j):
            return const[:, C_FWD + j * P:C_FWD + (j + 1) * P]

        def fwdu(j):
            return const[:, C_FWDU + j * P:C_FWDU + (j + 1) * P]

        def inv(j):
            return const[:, C_INV + j * P:C_INV + (j + 1) * P]

        def agg_inv(j):
            return const[:, C_AGG + j * P:C_AGG + (j + 1) * P]

        class Step:

            def __init__(self, s, h, batch, front=True, back=True):
                self.s, self.h, self.batch, self.front, self.back = s, h, batch, front, back
                self.first_use = s * STEP_USES - BACK_USES if back else 0
                self.first_bank = 2 if back and h == 1 else 0
                first_wt = 6 if front else 0
                self.at = {"fwd": 0, "wt": first_wt, "wfwd": first_wt + 2, "fwdu": 12 if back else 6,
                           "tw": 16 if front else 6}
                self.back_batch = batch if h == 1 else batch - 1
                self.static = isinstance(s, int)

            def use(self, kind, i):
                n = self.at[kind] + i
                return self.first_use + n, bank[(self.first_bank + n) % RING]

            def more_fronts(self):
                return not (self.static and self.s >= UNITS - 1)

        def steps(eng):
            yield Step(0, 0, 0, back=False)
            yield Step(1, 1, 0)
            yield Step(2, 0, 1)
            with eng.Fori(1, B - 1) as b:
                yield Step(2 * b + 1, 1, b)
                yield Step(2 * b + 2, 0, b + 1)
            yield Step(UNITS - 1, 1, B - 1)
            yield Step(UNITS, 0, B, front=False)

        x_d = io["x"].rearrange("b (t p) d -> b p t d", p=P)
        c_d = io["ctx"].rearrange("b (t p) d -> b p t d", p=P)
        x1_d = scratch["x1"].rearrange("b (t p) d -> b p t d", p=P)
        wgu_d = [io[n].rearrange("(b r) d -> b r d", r=PER) for n in ("wg", "wu")]
        wd_d = io["wd"].rearrange("(b p) i -> b p i", p=P)
        ws_gu_d = [scratch[n].rearrange("(b r) -> b r", r=PER) for n in ("ws_g", "ws_u")]
        ws_d_d = scratch["ws_d"].rearrange("(b p o) -> b p o", p=P, o=1)
        wT_gu_d = [scratch[n].rearrange("p k (b r) -> b p k r", r=PER) for n in ("wT_g", "wT_u")]
        wT_d_d = scratch["wT_d"].rearrange("p n (b d) -> b p n d", d=P)

        block = ctx.enter_context(nc.Block())

        @block.sync
        def _(sp):
            def load_weights(h, batch):
                for k, (o, n) in enumerate(ROWS):
                    sp.dma_start(wrow[h][k][0:n, :], wgu_d[h][batch, o:o + n, :]).then_inc(w_in[h][k], 16)
                if h == 0:
                    sp.dma_start(wd[:, :], wd_d[batch]).then_inc(wd_in, 16)

            def load_ctx(h, batch):
                sp.dma_start(ck[h][:, :, :], c_d[batch, :, :, h * HALF:(h + 1) * HALF]).then_inc(ctx_in[h], 16)

            sp.dma_start(xl[:, :, :], x_d[0]).then_inc(x_in, 16)
            load_ctx(0, 0)
            sp.dma_start(const[:, :], io["const"]).then_inc(const_in, 16)
            load_weights(0, 0)
            sp.dma_start(gx[:, :], io["g_x"].partition_broadcast(P)).then_inc(gx_in, 16)
            for q in steps(sp):
                s, h, batch = q.s, q.h, q.batch
                if q.front:
                    if q.more_fronts():
                        if h == 1:
                            sp.wait_ge(qn_done, 2 * (s + 1))
                            sp.sem_inc(held, 1)
                            sp.dma_start(xl[:, :, :], x_d[batch + 1]).then_inc(x_in, 16)
                        if q.back:
                            sp.wait_ge(wq_done, 3 * s)
                            sp.sem_inc(held, 1)
                        if h == 1:
                            sp.wait_ge(wdq_done, batch + 1)
                            sp.sem_inc(held, 1)
                        load_weights(1 - h, batch if h == 0 else batch + 1)
                        sp.wait_ge(u_done, s)
                        sp.sem_inc(held, 1)
                        if h == 0:
                            load_ctx(1, batch)
                        else:
                            load_ctx(0, batch + 1)
                    sp.wait_ge(x1_out[h], 16 * batch)
                    sp.sem_inc(held, 1)
                    sp.dma_start(xr[h][:, :, :], x_d[batch, :, :, h * HALF:(h + 1) * HALF]).then_inc(xr_in[h], 16)
                    sp.wait_ge(ws_done, s + 1)
                    sp.sem_inc(held, 1)
                    for k, (o, n) in enumerate(ROWS):
                        sp.dma_start(ws_gu_d[h][batch, o:o + n].rearrange("(p o) -> p o", o=1),
                                     ws[h][0:n, k:k + 1]).then_inc(ws_out[h], 16)
                    if h == 0:
                        sp.dma_start(ws_d_d[batch], ws[h][:, 3:4]).then_inc(ws_out[h], 16)
                if q.back:
                    hb = 1 - h
                    sp.wait_ge(ring_free, q.use("tw", 5)[0] + 1)
                    sp.sem_inc(held, 1)
                    sp.dma_start(wT_gu_d[hb][q.back_batch], stage[:, :, :]).then_inc(stage_out, 16)
                    sp.dma_start(wT_d_d[q.back_batch, :, hb * WD_HALF:(hb + 1) * WD_HALF, :],
                                 stage_d[:, :, :]).then_inc(stage_d_out, 16)
                    sp.wait_ge(x1_done, 2 * s)
                    sp.sem_inc(held, 1)
                    sp.dma_start(x1_d[q.back_batch, :, :, hb * HALF:(hb + 1) * HALF],
                                 xr[hb][:, :, :]).then_inc(x1_out[hb], 16)
            for h in range(2):
                sp.wait_ge(x1_out[h], 16 * B)
                sp.wait_ge(ws_out[h], (64 - 16 * h) * B)
            sp.wait_ge(stage_out, 16 * UNITS)
            sp.wait_ge(stage_d_out, 16 * UNITS)

        @block.gpsimd
        def _(pool):
            def row_rstd(batch):
                pool.wait_ge(veps_done, batch + 1)
                pool.tensor_tensor(rstd[:, :], veps[:, :], minus_half[:, :], ALU.pow).then_inc(rstd_done, 1)

            def fold(s, h, batch):
                pool.wait_ge(ctx_in[h], 16 * (batch + 1))
                pool.wait_ge(u_done, s)
                pool.tensor_tensor(kf[:, 0, :], ck[h][:, 0, :], ck[h][:, 1, :], ALU.add).then_inc(fold_done, 1)
                pool.tensor_tensor(kf[:, 1, :], ck[h][:, 0, :], ck[h][:, 1, :], ALU.subtract).then_inc(fold_done, 1)
                pool.wait_ge(qn_done, 2 * (s + 1))
                pool.tensor_tensor(qf[:, 0, :], qn[:, 0, :], qn[:, 1, :], ALU.add).then_inc(fold_done, 1)
                pool.tensor_tensor(qf[:, 1, :], qn[:, 0, :], qn[:, 1, :], ALU.subtract).then_inc(fold_done, 1)

            pool.memset(minus_half[:, :], -0.5).then_inc(set_up, 1)
            pool.memset(magic[:, 0:1], MAGIC).then_inc(set_up, 1)
            pool.memset(magic[:, 1:2], -MAGIC).then_inc(set_up, 1)
            pool.memset(am[:, :], 0.0).then_inc(set_up, 1)
            pool.memset(wdq[:, I:NI * P], 0.0).then_inc(set_up, 1)
            pool.wait_ge(set_up, 5)
            row_rstd(0)
            fold(0, 0, 0)
            for q in steps(pool):
                s, h, batch = q.s, q.h, q.batch
                if h == 1 and q.more_fronts():
                    row_rstd(batch + 1)
                if q.back:
                    pool.wait_ge(agg_done, 2 * (s - 1))
                    pool.wait_ge(ring_free, q.use("wfwd", 1)[0] + 1)
                    for k in range(2):
                        pool.tensor_tensor(T0[:, k], US[1 - h][:, k], WS[:, 0], ALU.mult).then_inc(t0_done, 1)
                    pool.wait_ge(aggp_done, 4 * s)
                    for k in (1, 0):
                        pool.tensor_tensor(S0[:, k], S0[:, k], S1[:, k], ALU.add).then_inc(add_done, 1)
                if q.front and q.more_fronts():
                    fold(s + 1, 1 - h, batch if h == 0 else batch + 1)
                if q.front:
                    if h == 0:
                        pool.wait_ge(rw_done, s + 1)
                        pool.sem_inc(held, 1)
                        pool.tensor_scalar(wd[:, :], wd[:, :], rw[h][:, 3:4], MAGIC, ALU.mult, ALU.add).then_inc(yd_done, 1)
                    if q.back:
                        pool.wait_ge(ring_full, q.use("tw", 5)[0] + 1)
                        pool.sem_inc(held, 1)
                    for k, (o, n) in enumerate(ROWS):
                        pool.wait_ge(y_done, 3 * s + k + 1)
                        pool.sem_inc(held, 1)
                        pool.tensor_scalar(wq[k][0:n, :], wrow[h][k][0:n, :], -MAGIC, 1.0, ALU.add, ALU.mult).then_inc(wq_done, 1)
                    if h == 0:
                        pool.wait_ge(yd_done, batch + 1)
                        pool.sem_inc(held, 1)
                        pool.tensor_scalar(wdq[:, 0:I], wd[:, :], -MAGIC, 1.0, ALU.add, ALU.mult).then_inc(wdq_done, 1)

        @block.scalar
        def _(act):
            def normalise(s, h, batch):
                act.wait_ge(ln_done, batch + 1)
                act.wait_ge(fold_done, 4 * s)
                for t in range(2):
                    act.activation(qn[:, t, :], xl[:, t, h * HALF:(h + 1) * HALF], ACT.Identity,
                                   bias=nmr[:, t:t + 1], scale=rstd[:, t:t + 1]).then_inc(qn_done, 1)

            def empty(q, kind, i, out, src=None):
                n, b = q.use(kind, i)
                act.wait_ge(ring_full, n + 1)
                act.activation(out, b[:, :] if src is None else src(b), ACT.Copy).then_inc(ring_free, 1)

            def empty_weights(q, g):
                if g == 0:
                    act.wait_ge(stage_out, 16 * (q.s - 1))
                    act.wait_ge(stage_d_out, 16 * (q.s - 1))
                if g < 3:
                    o, n = ROWS[g]
                    empty(q, "tw", g, stage[:, :, o:o + n],
                          lambda b: b[:, :].bitcast(BF16).rearrange("p (k r) -> p k r", r=P)[:, :, 0:n])
                else:
                    a, e = WD_GROUPS[g - 3]
                    empty(q, "tw", g, stage_d[:, a:e, :],
                          lambda b: b[:, :].bitcast(BF16)[:, 0:(e - a) * P].rearrange("p (k r) -> p k r", r=P))

            def round_rows(h, k):
                n = ROWS[k][1]
                act.activation(wrow[h][k][0:n, :], wrow[h][k][0:n, :], ACT.Identity,
                               bias=magic[0:n, 0:1], scale=rw[h][0:n, k:k + 1]).then_inc(y_done, 1)

            act.wait_ge(const_in, 16)
            act.activation(identb[:, :], ident, ACT.Copy).then_inc(ident_done, 1)
            act.wait_ge(gx_in, 16)
            act.activation(gt[:, :], gx[:, :], ACT.Tanh).then_inc(gate_done, 1)
            act.wait_ge(set_up, 5)
            normalise(0, 0, 0)
            for q in steps(act):
                s, h, batch = q.s, q.h, q.batch
                if q.front:
                    act.wait_ge(prod_done, 2 * s)
                    for i in range(2):
                        empty(q, "fwd", i, QS[:, i, :])
                    if q.back:
                        act.wait_ge(aggp_done, 4 * (s - 1))
                        act.wait_ge(t0_done, 2 * (s - 1))
                    for i in range(4):
                        empty(q, "fwd", 2 + i, KS[h][:, i // 2, i % 2, :])
                if q.back:
                    for i in range(2):
                        empty(q, "wt", i, WT[:, i, :])
                if q.front:
                    act.wait_ge(rw_done, s + 1)
                    round_rows(h, 0)
                if q.back:
                    act.wait_ge(aggp_done, 4 * (s - 1))
                    act.wait_ge(t0_done, 2 * (s - 1))
                    for i in range(4):
                        empty(q, "wfwd", i, WS[:, i // 2, i % 2, :])
                if q.front:
                    act.wait_ge(corr_done, 2 * s + 1)
                    act.activation(ODD[:, :, :], corr[1][:, :, :], ACT.Copy).then_inc(odd_done, 1)
                    if q.more_fronts():
                        normalise(s + 1, 1 - h, batch if h == 0 else batch + 1)
                    for i in range(4):
                        empty(q, "fwdu", i, US[h][:, i // 2, i % 2, :])
                    act.wait_ge(nmax_done, s + 1)
                    for n in range(HEADS):
                        act.activation(W[:, n, :], CR[:, n, :], ACT.Exp, bias=nmax[:, n:n + 1]).then_inc(exp_done, 1)
                if q.back:
                    for g in range(4):
                        empty_weights(q, g)
                if q.front:
                    round_rows(h, 1)
                if q.back:
                    for g in range(4, 6):
                        empty_weights(q, g)
                if q.front:
                    round_rows(h, 2)

        @block.vector
        def _(dve):
            def row_stats(batch):
                dve.wait_ge(x_in, 16 * (batch + 1))
                for t in range(2):
                    for c in range(2):
                        dve.bn_stats(bn[:, t, c, :], xl[:, t, c * HALF:(c + 1) * HALF]).then_inc(bn_done, 1)
                dve.wait_ge(bn_done, 4 * (batch + 1))
                dve.sem_inc(held, 1)
                for t in range(2):
                    dve.bn_aggr(mv[:, t, :], bn[:, t, :, :]).then_inc(mv_done, 1)
                dve.wait_ge(mv_done, 2 * (batch + 1))
                dve.tensor_scalar(veps[:, :], mv[:, :, 1], LN_EPS, None, ALU.add).then_inc(veps_done, 1)
                dve.wait_ge(rstd_done, batch + 1)
                dve.scalar_tensor_tensor(out=nmr[:, :], in0=mv[:, :, 0], scalar=-1.0, in1=rstd[:, :],
                                         op0=ALU.mult, op1=ALU.mult).then_inc(ln_done, 1)

            row_stats(0)
            dve.wait_ge(set_up, 5)
            dve.wait_ge(const_in, 16)
            for q in steps(dve):
                s, h, batch = q.s, q.h, q.batch
                if q.front:
                    seen = 7 * batch + (4 if h == 1 else 0)
                    if h == 0:
                        dve.wait_ge(wd_in, 16 * (batch + 1))
                        dve.tensor_reduce(am[:, 3:4], wd[:, :], AX_X, ALU.max,
                                          apply_absolute_value=True).then_inc(am_done, 1)
                    for k, (o, n) in enumerate(ROWS):
                        dve.wait_ge(w_in[h][k], 16 * (batch + 1))
                        dve.tensor_reduce(am[0:n, k:k + 1], wrow[h][k][0:n, :], AX_X, ALU.max,
                                          apply_absolute_value=True).then_inc(am_done, 1)
                    n = 4 if h == 0 else 3
                    dve.wait_ge(ws_out[h], (64 - 16 * h) * batch)
                    dve.wait_ge(am_done, seen + n)
                    dve.tensor_scalar(ws[h][:, 0:n], am[:, 0:n], 1.0 / QMAX, 1e-8, ALU.mult, ALU.max).then_inc(ws_done, 1)
                    dve.wait_ge(ws_done, s + 1)
                    dve.reciprocal(rw[h][:, 0:n], ws[h][:, 0:n]).then_inc(rw_done, 1)
                    if q.back:
                        dve.wait_ge(corr_done, 2 * s)
                    for k in range(2):
                        dve.wait_ge(ring_free, q.use("fwd", 3 + 2 * k)[0] + 1)
                        dve.tensor_tensor(PT[:, k], QS[:, :, :], KS[h][:, k], ALU.mult).then_inc(prod_done, 1)
                    if h == 1 and q.more_fronts():
                        row_stats(batch + 1)
                if q.back:
                    hb = 1 - h
                    dve.wait_ge(agg_done, 2 * (s - 1))
                    for out, spec, half in ((S0, KS, 0), (S1, US, 1)):
                        if out is S0:
                            dve.wait_ge(ring_free, q.use("wfwd", 1)[0] + 1)
                        if out is S1:
                            dve.wait_ge(ring_free, q.use("wfwd", 3)[0] + 1)
                        for k in range(2):
                            dve.tensor_tensor(out[:, k], spec[hb][:, k], WS[:, half], ALU.mult).then_inc(aggp_done, 1)
                if q.front:
                    dve.wait_ge(exp_done, HEADS * s)
                    dve.wait_ge(corr_done, 2 * (s + 1))
                    dve.wait_ge(odd_done, s + 1)
                    for k, op in enumerate((ALU.add, ALU.subtract)):
                        dve.tensor_tensor(CR[:, :, k * P:(k + 1) * P], corr[0][:, :, :], ODD[:, :, :], op).then_inc(cr_done, 1)
                    dve.wait_ge(cr_done, 2 * (s + 1))
                    dve.sem_inc(held, 1)
                    for n in range(HEADS):
                        dve.max(M1[:, n, :], CR[:, n, :]).then_inc(top8_done, 1)
                    dve.wait_ge(top8_done, HEADS * (s + 1))
                    dve.tensor_scalar(nmax[:, :], M1[:, :, 0], -1.0, None, ALU.mult).then_inc(nmax_done, 1)
                    for n in range(HEADS):
                        dve.match_replace(R[:, n, :], M1[:, n, :], CR[:, n, :], TAKEN).then_inc(rep8_done, 1)
                    dve.wait_ge(rep8_done, HEADS * (s + 1))
                    dve.sem_inc(held, 1)
                    for n in range(HEADS):
                        dve.max(M2[:, n, :], R[:, n, :]).then_inc(top16_done, 1)
                    dve.wait_ge(top16_done, HEADS * (s + 1))
                    dve.memset(M2[:, :, TOPK - 8:8], TAKEN).then_inc(pad_done, 1)
                    dve.wait_ge(pad_done, s + 1)
                    dve.sem_inc(held, 1)
                    for n in range(HEADS):
                        dve.match_replace(R[:, n, :], M2[:, n, :], R[:, n, :], TAKEN).then_inc(rep16_done, 1)
                    for n in range(HEADS):
                        dve.wait_ge(rep16_done, HEADS * s + n + 1)
                        dve.wait_ge(exp_done, HEADS * s + n + 1)
                        dve.scalar_tensor_tensor(out=W[:, n, :], in0=R[:, n, :], scalar=-1.0e38, in1=W[:, n, :],
                                                 op0=ALU.is_lt, op1=ALU.mult,
                                                 accum_out=Z[:, n:n + 1]).then_inc(mask_done, 1)
                    dve.wait_ge(mask_done, HEADS * (s + 1))
                    dve.reciprocal(rz[:, :], Z[:, :]).then_inc(rz_done, 1)
                    dve.wait_ge(rz_done, s + 1)
                    for n in range(HEADS):
                        dve.tensor_scalar(W[:, n, :], W[:, n, :], rz[:, n:n + 1], None, ALU.mult).then_inc(norm_done, 1)
                if q.back:
                    dve.wait_ge(gate_done, 1)
                    dve.wait_ge(xr_in[hb], 16 * (q.back_batch + 1))
                    for n, t in enumerate((1, 0)):
                        dve.wait_ge(agg_done, 2 * (s - 1) + n + 1)
                        dve.scalar_tensor_tensor(out=xr[hb][:, t, :], in0=agg[t][:, :], scalar=gt[:, 0:1],
                                                 in1=xr[hb][:, t, :], op0=ALU.mult, op1=ALU.add).then_inc(x1_done, 1)

        @block.tensor
        def _(pe):
            def ring(q, kind, i):
                n, b = q.use(kind, i)
                if not (isinstance(n, int) and n < RING):
                    pe.wait_ge(ring_free, n + 1 - RING)
                return b

            def transpose_weights(q, g):
                if g == 0:
                    pe.wait_ge(wq_done, 3 * q.s)
                    pe.wait_ge(wdq_done, q.back_batch + 1)
                b = ring(q, "tw", g)[:, :].bitcast(BF16).rearrange("p (k r) -> p k r", r=P)
                if g < 3:
                    n = ROWS[g][1]
                    for k in range(NK):
                        mm = pe.transpose(b[:, k, 0:n], wq[g][0:n, k * P:(k + 1) * P], identb[0:n, 0:n])
                else:
                    a, e = WD_GROUPS[g - 3]
                    for k in range(a, e):
                        c = (1 - q.h) * WD_HALF + k
                        mm = pe.transpose(b[:, k - a, :], wdq[:, c * P:(c + 1) * P], identb[:, :])
                mm.then_inc(ring_full, 1)

            pe.wait_ge(set_up, 5)
            pe.wait_ge(ident_done, 1)
            for q in steps(pe):
                s, h, batch = q.s, q.h, q.batch
                if q.front:
                    pe.wait_ge(fold_done, 4 * (s + 1))
                    for i in range(6):
                        src = qf if i < 2 else kf
                        pe.matmul(ring(q, "fwd", i)[:, :], fwd((0, 1, 0, 1, 2, 3)[i]), src[:, i % 2, :],
                                  start=True, stop=True).then_inc(ring_full, 1)
                if q.back:
                    pe.wait_ge(norm_done, HEADS * s)
                    for half in range(2):
                        b = ring(q, "wt", half)
                        for n in range(HEADS):
                            mm = pe.transpose(b[:, n * P:(n + 1) * P], W[:, n, half * P:(half + 1) * P], ident)
                        mm.then_inc(ring_full, 1)
                    for i in range(4):
                        if i % 2 == 0:
                            pe.wait_ge(ring_free, q.use("wt", i // 2)[0] + 1)
                        pe.matmul(ring(q, "wfwd", i)[:, :], fwd(i % 2), WT[:, i // 2, :],
                                  start=True, stop=True).then_inc(ring_full, 1)
                if q.front:
                    pe.wait_ge(prod_done, 2 * (s + 1))
                    pe.wait_ge(odd_done, s)
                    pe.wait_ge(cr_done, 2 * s)
                    for eo in (1, 0):
                        for n in range(HEADS):
                            for kind in range(2):
                                mm = pe.matmul(corr[eo][:, n, :], PT[:, kind, eo, n * P:(n + 1) * P], inv(2 * kind + eo),
                                               start=(kind == 0), stop=(kind == 1))
                        mm.then_inc(corr_done, 1)
                if q.front:
                    for i in range(4):
                        pe.matmul(ring(q, "fwdu", i)[:, :], fwdu(i), ck[h][:, 1, :],
                                  start=True, stop=True).then_inc(ring_full, 1)
                    pe.wait_ge(ring_full, q.use("fwdu", 3)[0] + 1)
                    pe.nop().then_inc(u_done, 1)
                if q.back:
                    for g in range(4):
                        transpose_weights(q, g)
                if q.back:
                    pe.wait_ge(x1_done, 2 * (s - 1))
                    pe.wait_ge(t0_done, 2 * s)
                    for j in range(4):
                        pe.matmul(agg[1][:, :], agg_inv(j), T0[:, j // 2, j % 2, :], start=(j == 0), stop=False)
                    pe.wait_ge(add_done, 2 * s - 1)
                    pe.matmul(agg[1][:, :], const[:, C_SUM:C_SUM + P], S0[:, 1, 0, :],
                              start=False, stop=True).then_inc(agg_done, 1)
                    for g in range(4, 6):
                        transpose_weights(q, g)
                    pe.wait_ge(add_done, 2 * s)
                    for j in range(4):
                        mm = pe.matmul(agg[0][:, :], agg_inv(j), S0[:, j // 2, j % 2, :], start=(j == 0), stop=(j == 3))
                    mm.then_inc(agg_done, 1)


def feed_forward(nc, sems, io, scratch, out):
    B, L, D = io["x"].shape
    I = io["wg"].shape[0]
    NK = D // P
    NI = -(-I // P)
    LAST = I - (NI - 1) * P
    PER, _ = row_tiles(I, B)

    ctx = ExitStack()
    with ctx:
        def sb(name, shape, dt=F32):
            return ctx.enter_context(nc.sbuf_tensor(name, shape, dt))

        def sem(name):
            return sems.enter_context(nc.semaphore("f_" + name))

        wgT = sb("wgT", [P, NK, I], BF16)
        wuT = sb("wuT", [P, NK, I], BF16)
        wdT = sb("wdT", [P, NI, D], BF16)
        hid = [sb(f"hid{i}", [P, NI, L]) for i in range(2)]
        xin = sb("xin", [P, D])
        qrow = sb("qrow", [P, 2, D], BF16)
        qT = sb("qT", [P, NK, L], BF16)
        res = sb("res", [P, D])
        wn = sb("wn", [P, D])
        wsd = sb("wsd", [P, D])
        gs = [sb(f"gs{i}", [P, L]) for i in range(3)]
        mx = sb("mx", [P, L])
        rb = sb("rb", [P, L])
        sbc = [sb(f"sbc{i}", [P, L]) for i in range(2)]
        identf = sb("identf", [P, P])
        identb = sb("identb2", [P, P], BF16)
        ones = sb("ones", [P, P])
        dg = sb("dg2", [P, 2, P])
        wsgu = sb("wsgu", [P, 2, NI])
        wsg, wsu = wsgu[:, 0, :], wsgu[:, 1, :]
        small = sb("small", [P, 64])
        gf = small[:, 0:1]
        gt = small[:, 1:2]
        magic = small[:, 2:3]
        minus_half = small[:, 3:4]
        bn = small[:, 4:16].rearrange("p (c k) -> p c k", c=2)
        mv = small[:, 16:18]
        veps = small[:, 18:19]
        rstd = small[:, 19:20]
        ms = small[:, 20:21]
        ms2 = small[:, 21:22]
        r2 = small[:, 22:23]
        a_ = small[:, 23:24]
        amx = small[:, 24:25]
        rs = small[:, 25:26]
        sc = small[:, 26:27]
        smax = small[:, 28:29]
        hm = small[:, 30:32]
        s2 = small[:, 32:34]
        rs2 = small[:, 34:36]
        rr = small[:, 36:38]
        s2raw = small[:, 38:40]
        scol = [small[:, 40 + 2 * i:42 + 2 * i] for i in range(2)]
        s2g = [small[:, 44 + 2 * i:46 + 2 * i] for i in range(2)]

        bank = [ctx.enter_context(nc.psum_tensor(f"gu{i}", [P, 2, L], F32)) for i in range(RING)]
        down = [ctx.enter_context(nc.psum_tensor(f"down{i}", [P, HALF], F32)) for i in range(3)]
        misc = ctx.enter_context(nc.psum_tensor("misc", [P, 512], F32))
        DOWN_BANK = (0, 1, 2, 1)

        held = sem("held")
        const_in = sem("const_in")
        scale_in = sem("scale_in")
        gu_in = [sem(f"gu_in{c}") for c in range(B)]
        wd_in = sem("wd_in")
        x_in = sem("x_in")
        x_second_in = sem("x_second_in")
        res_in = sem("res_in")
        y_out = sem("y_out")
        set_up = sem("set_up")
        ident_done = sem("ident_done")
        gate_done = sem("gate_done")
        prep = {n: sem("p_" + n) for n in ("bn", "mv", "veps", "rstd", "ms", "ms2", "r2", "a", "u", "amx", "smax", "s",
                                           "rs", "sc", "y", "q")}
        dgs_done = sem("dgs_done")
        misc_full = sem("misc_full")
        misc_free = sem("misc_free")
        gu_full = sem("gu_full")
        gs_done = sem("gs_done")
        si_done = sem("si_done")
        hid_done = sem("hid_done")
        abs_done = sem("abs_done")
        mx_done = sem("mx_done")
        scaled_done = sem("scaled_done")
        magic_done = sem("magic_done")
        q2_done = sem("q2_done")
        s2raw_done = sem("s2raw_done")
        s2_done = sem("s2_done")
        rs2_done = sem("rs2_done")
        rr_done = sem("rr_done")
        s2g_done = sem("s2g_done")
        dgr_done = sem("dgr_done")
        down_full = sem("down_full")
        down_scaled = sem("down_scaled")
        y_done = sem("y_done")

        x1_d = scratch["x1"].rearrange("b (t p) d -> b t p d", p=P)
        out_d = out.rearrange("b (t p) d -> b t p d", p=P)

        def rows(i):
            return P if i < NI - 1 else LAST

        def q2(par, i):
            return hid[par][:, i, :].bitcast(BF16).rearrange("p (t k) -> p t k", t=2)[:, :, 0:P]

        class Step:
            def __init__(self, b, par, hidden=True, down=True, more=True):
                self.b, self.par, self.hidden, self.down, self.more = b, par, hidden, down, more
                self.first_bank = 2 * par

            def use(self, i):
                return NI * self.b + i, bank[(self.first_bank + i) % RING]

        def steps(eng):
            yield Step(0, 0, down=False)
            yield Step(1, 1)
            yield Step(2, 0)
            with eng.Fori(1, (B - 2) // 2) as k:
                yield Step(2 * k + 1, 1)
                yield Step(2 * k + 2, 0)
            yield Step(B - 1, 1, more=False)
            yield Step(B, 0, hidden=False, more=False)

        def misc_use(b, n):
            if n < 3:
                return n + 1 if isinstance(b, int) and b == 0 else 5 * b - 1 + n
            return 5 * b + n + 1 if isinstance(b, int) and b == B - 1 else 5 * b + n + 4

        PREP_FROM = (2, 12)

        block = ctx.enter_context(nc.Block())

        @block.sync
        def _(sp):
            def load_x(b, t):
                if not (isinstance(b, int) and b == 0):
                    sp.wait_ge(prep["q"], 2 * b + t)
                    sp.sem_inc(held, 1)
                sp.dma_start(xin[:, :], x1_d[b, t]).then_inc(x_in, 16)

            load_x(0, 0)
            sp.dma_start(wn[:, :], io["w_rms"].partition_broadcast(P)).then_inc(const_in, 16)
            sp.dma_start(identf[:, :], io["const"][:, C_IDENT:C_END]).then_inc(const_in, 16)
            sp.dma_start(gf, io["g_f"].partition_broadcast(P)).then_inc(const_in, 16)
            sp.dma_start(res[:, :], x1_d[0, 1]).then_inc(x_second_in, 16)
            sp.wait_ge(set_up, 4)
            full = (NI - 1) * P
            for half, src in enumerate((scratch["ws_g"], scratch["ws_u"])):
                cols = slice(half * P, (half + 1) * P)
                sp.dma_start(rb[0:NI - 1, cols], src[0:full].rearrange("(n p) -> n p", p=P)).then_inc(scale_in, 16)
                sp.dma_start(rb[NI - 1:NI, half * P:half * P + LAST],
                             src[full:I].rearrange("(o p) -> o p", o=1)).then_inc(scale_in, 16)
            for c in range(B):
                for tile, src in ((wgT, scratch["wT_g"]), (wuT, scratch["wT_u"])):
                    sp.dma_start(tile[:, :, c * PER:(c + 1) * PER], src[:, :, c * PER:(c + 1) * PER]).then_inc(gu_in[c], 16)
            sp.dma_start(wdT[:, :, :], scratch["wT_d"]).then_inc(wd_in, 16)
            sp.dma_start(wsd[:, :], scratch["ws_d"].partition_broadcast(P)).then_inc(wd_in, 16)
            for q in steps(sp):
                b = q.b
                if q.more:
                    load_x(b + 1, 0)
                    load_x(b + 1, 1)
                if q.down:
                    for t in range(2):
                        if not (isinstance(b, int) and b == 1 and t == 0):
                            sp.wait_ge(y_out, 16 * (2 * (b - 1) + t))
                            sp.sem_inc(held, 1)
                        sp.dma_start(res[:, :], x1_d[b - 1, t]).then_inc(res_in, 16)
                        sp.wait_ge(y_done, 4 * (b - 1) + 2 * t + 2)
                        sp.sem_inc(held, 1)
                        sp.dma_start(out_d[b - 1, t], res[:, :]).then_inc(y_out, 16)
            sp.wait_ge(y_out, 16 * 2 * B)

        @block.gpsimd
        def _(pool):
            pool.memset(rb[:, :], 0.0).then_inc(set_up, 1)
            pool.memset(minus_half, -0.5).then_inc(set_up, 1)
            pool.memset(magic, MAGIC).then_inc(set_up, 1)
            pool.memset(ones[:, :], 1.0).then_inc(set_up, 1)
            pool.wait_ge(set_up, 4)

            def layer_norm_root(n):
                pool.wait_ge(prep["veps"], n + 1)
                pool.tensor_tensor(rstd, veps, minus_half, ALU.pow).then_inc(prep["rstd"], 1)

            def rms_norm_root(n):
                pool.wait_ge(prep["ms2"], n + 1)
                pool.tensor_tensor(r2, ms2, minus_half, ALU.pow).then_inc(prep["r2"], 1)

            def scale_hidden(b, par, i):
                t = hid[par][0:rows(i), i, :]
                pool.tensor_tensor(t, t, rb[0:rows(i), :], ALU.mult).then_inc(scaled_done, 1)

            def take_magic_off(b, par, i):
                n = rows(i)
                pool.wait_ge(magic_done, NI * b + i + 1)
                pool.sem_inc(held, 1)
                pool.tensor_scalar(q2(par, i)[0:n, :, :], hid[par][0:n, i, :].rearrange("p (t k) -> p t k", t=2),
                                   -MAGIC, 1.0, ALU.add, ALU.mult).then_inc(q2_done, 1)

            def round_input(n, t, buf):
                pool.wait_ge(prep["y"], n + 1)
                pool.sem_inc(held, 1)
                pool.tensor_scalar(qrow[:, t, :], buf[:, :], -MAGIC, 1.0, ALU.add, ALU.mult).then_inc(prep["q"], 1)

            for n in range(2):
                layer_norm_root(n)
                rms_norm_root(n)
                round_input(n, n, res if n else xin)
            for q in steps(pool):
                b, par = q.b, q.par
                if q.down:
                    pool.wait_ge(misc_free, misc_use(b - 1, 4) + 1)
                for i in range(NI + 1):
                    if q.down and i < NI:
                        scale_hidden(b - 1, 1 - par, i)
                    if q.down and i > 0:
                        take_magic_off(b - 1, 1 - par, i - 1)
                    if q.more:
                        for t in range(2):
                            n = 2 * (b + 1) + t
                            if i == PREP_FROM[t] + 1:
                                layer_norm_root(n)
                            if i == PREP_FROM[t] + 4:
                                rms_norm_root(n)
                            if i == PREP_FROM[t] + 7:
                                round_input(n, t, xin)

        @block.scalar
        def _(act):
            def round_input(n, buf):
                act.wait_ge(prep["sc"], n + 1)
                act.activation(buf[:, :], buf[:, :], ACT.Identity, bias=magic, scale=sc).then_inc(prep["y"], 1)

            def empty_misc(b, n, out, src):
                act.wait_ge(misc_full, misc_use(b, n) + 1)
                act.activation(out, src, ACT.Copy).then_inc(misc_free, 1)

            def empty_input(b, par):
                empty_misc(b, 0, sbc[par][:, :], misc[:, 0:L])
                for t in range(2):
                    empty_misc(b, 1 + t, qT[:, :, t * P:(t + 1) * P],
                               misc[:, :].bitcast(BF16).rearrange("p (k r) -> p k r", r=P))

            def magnitude(q, i):
                n = rows(i)
                act.wait_ge(hid_done, NI * q.b + i + 1)
                act.activation(gs[i % 3][0:n, :], hid[q.par][0:n, i, :], ACT.Abs).then_inc(abs_done, 1)

            act.wait_ge(const_in, 48)
            act.activation(identb[:, :], identf[:, :], ACT.Copy).then_inc(ident_done, 1)
            act.activation(gt, gf, ACT.Tanh).then_inc(gate_done, 1)
            act.wait_ge(set_up, 4)
            act.wait_ge(misc_full, 1)
            act.activation(wsgu[:, :, :], misc[:, 0:2 * NI].rearrange("p (h n) -> p h n", h=2), ACT.Copy).then_inc(misc_free, 1)
            round_input(0, xin)
            round_input(1, res)
            empty_input(0, 0)
            for q in steps(act):
                b, par = q.b, q.par
                for i in range(NI):
                    n = rows(i)
                    if q.hidden:
                        act.wait_ge(gs_done, NI * b + i + 1)
                        act.activation(gs[i % 3][0:n, :], gs[i % 3][0:n, :], ACT.Silu,
                                       scale=wsg[0:n, i:i + 1]).then_inc(si_done, 1)
                    if q.down:
                        act.wait_ge(scaled_done, NI * (b - 1) + i + 1)
                        t = hid[1 - par][0:n, i, :]
                        act.activation(t, t, ACT.Identity, bias=magic[0:n, :]).then_inc(magic_done, 1)
                    if q.hidden and i > 0:
                        magnitude(q, i - 1)
                    if q.more and i - 6 in PREP_FROM:
                        round_input(2 * (b + 1) + PREP_FROM.index(i - 6), xin)
                if q.hidden:
                    magnitude(q, NI - 1)
                if q.more:
                    empty_input(b + 1, 1 - par)
                if q.hidden:
                    empty_misc(b, 4, rb[:, :], misc[:, 0:L])

        @block.vector
        def _(dve):
            def link(ins, s, n):
                ins.then_inc(s, 1)
                dve.wait_ge(s, n)

            def prepare(n, t, par, piece, buf):
                if piece == 0:
                    for c in range(2):
                        dve.bn_stats(bn[:, c, :], buf[:, c * HALF:(c + 1) * HALF]).then_inc(prep["bn"], 1)
                    dve.wait_ge(prep["bn"], 2 * (n + 1))
                    dve.sem_inc(held, 1)
                    link(dve.bn_aggr(mv, bn), prep["mv"], n + 1)
                    dve.tensor_scalar(veps, mv[:, 1:2], LN_EPS, None, ALU.add).then_inc(prep["veps"], 1)
                if piece == 1:
                    dve.scalar_tensor_tensor(out=buf[:, :], in0=buf[:, :], scalar=mv[:, 0:1], in1=wn[:, :],
                                             op0=ALU.subtract, op1=ALU.mult).then_inc(prep["u"], 1)
                if piece == 2:
                    dve.wait_ge(prep["u"], n + 1)
                    dve.tensor_reduce(amx, buf[:, :], AX_X, ALU.max, apply_absolute_value=True).then_inc(prep["amx"], 1)
                if piece == 3:
                    dve.wait_ge(prep["rstd"], n + 1)
                    link(dve.scalar_tensor_tensor(out=ms, in0=mv[:, 1:2], scalar=rstd, in1=rstd,
                                                  op0=ALU.mult, op1=ALU.mult), prep["ms"], n + 1)
                    dve.tensor_scalar(ms2, ms, RMS_EPS, None, ALU.add).then_inc(prep["ms2"], 1)
                if piece == 4:
                    dve.wait_ge(prep["r2"], n + 1)
                    link(dve.tensor_tensor(a_, rstd, r2, ALU.mult), prep["a"], n + 1)
                    dve.wait_ge(prep["amx"], n + 1)
                    link(dve.tensor_tensor(smax, amx, a_, ALU.mult), prep["smax"], n + 1)
                    s = scol[par][:, t:t + 1]
                    link(dve.tensor_scalar(s, smax, 1.0 / QMAX, 1e-8, ALU.mult, ALU.max), prep["s"], n + 1)
                    link(dve.reciprocal(rs, s), prep["rs"], n + 1)
                    dve.tensor_tensor(sc, a_, rs, ALU.mult).then_inc(prep["sc"], 1)
                    dve.tensor_scalar(dg[:, t, :], identf[:, :], s, None, ALU.mult).then_inc(dgs_done, 1)

            def hidden(q, i):
                b, par, n = q.b, q.par, rows(i)
                use, bk = q.use(i)
                dve.wait_ge(si_done, use + 1)
                t = hid[par][0:n, i, :]
                dve.scalar_tensor_tensor(out=t, in0=bk[0:n, 1, :], scalar=wsu[0:n, i:i + 1], in1=gs[i % 3][0:n, :],
                                         op0=ALU.mult, op1=ALU.mult).then_inc(hid_done, 1)

            def running_max(q, i):
                n = rows(i)
                dve.wait_ge(abs_done, NI * q.b + i + 1)
                if i == 0:
                    dve.tensor_copy(mx[:, :], gs[0][:, :]).then_inc(mx_done, 1)
                else:
                    dve.wait_ge(mx_done, NI * q.b + i)
                    dve.tensor_tensor(mx[0:n, :], gs[i % 3][0:n, :], mx[0:n, :], ALU.max).then_inc(mx_done, 1)

            def project_out(b, quarter, par):
                t, c = quarter // 2, quarter % 2
                n = 4 * b + quarter
                bk = down[DOWN_BANK[quarter]]
                cols = slice(c * HALF, (c + 1) * HALF)
                dve.wait_ge(down_full, n + 1)
                link(dve.scalar_tensor_tensor(out=bk[:, :], in0=bk[:, :], scalar=s2g[par][:, t:t + 1],
                                              in1=wsd[:, cols], op0=ALU.mult, op1=ALU.mult), down_scaled, n + 1)
                if c == 0:
                    dve.wait_ge(res_in, 16 * (2 * b + t + 1))
                dve.tensor_tensor(res[:, cols], bk[:, :], res[:, cols], ALU.add).then_inc(y_done, 1)

            PIECE_AT = {0: 0, 1: 1, 2: 2, 3: 3, 5: 4}

            dve.wait_ge(const_in, 48)
            dve.wait_ge(set_up, 4)
            for t in range(2):
                dve.wait_ge(x_second_in if t else x_in, 16)
                for piece in range(5):
                    prepare(t, t, 0, piece, res if t else xin)
            dve.wait_ge(misc_free, 1)
            for q in steps(dve):
                b, par = q.b, q.par
                if q.down:
                    dve.wait_ge(misc_free, misc_use(b - 1, 4) + 1)
                if q.hidden:
                    dve.wait_ge(misc_free, misc_use(b, 0) + 1)
                for i in range(NI + 2):
                    if q.hidden and i < NI:
                        n = rows(i)
                        use, bk = q.use(i)
                        if i > 2:
                            dve.wait_ge(mx_done, use - 2)
                        elif not (isinstance(b, int) and b == 0):
                            dve.wait_ge(mx_done, NI * b)
                        dve.wait_ge(gu_full, use + 1)
                        dve.tensor_tensor(gs[i % 3][0:n, :], bk[0:n, 0, :], sbc[par][0:n, :], ALU.mult).then_inc(gs_done, 1)
                    if q.hidden and 0 < i <= NI:
                        hidden(q, i - 1)
                    if q.hidden and i > 1:
                        running_max(q, i - 2)
                    if q.more:
                        for t in range(2):
                            if i - PREP_FROM[t] in PIECE_AT:
                                n = 2 * (b + 1) + t
                                piece = PIECE_AT[i - PREP_FROM[t]]
                                if piece == 0:
                                    dve.wait_ge(x_in, 16 * n)
                                prepare(n, t, 1 - par, piece, xin)
                if q.down:
                    dve.wait_ge(wd_in, 32)
                    project_out(b - 1, 0, 1 - par)
                if q.hidden:
                    s = scol[par]
                    dve.wait_ge(misc_full, misc_use(b, 3) + 1)
                    link(dve.tensor_reduce(hm, misc[:, 0:L].rearrange("p (t k) -> p t k", t=2), AX_X, ALU.max),
                         misc_free, misc_use(b, 3) + 1)
                    link(dve.tensor_tensor(s2raw, hm, s, ALU.mult), s2raw_done, b + 1)
                    link(dve.tensor_scalar(s2, s2raw, 1.0 / QMAX, 1e-8, ALU.mult, ALU.max), s2_done, b + 1)
                    link(dve.reciprocal(rs2, s2), rs2_done, b + 1)
                    link(dve.tensor_tensor(rr, rs2, s, ALU.mult), rr_done, b + 1)
                    for t in range(2):
                        dve.tensor_scalar(dg[:, t, :], identf[:, :], rr[:, t:t + 1], None, ALU.mult).then_inc(dgr_done, 1)
                    dve.wait_ge(gate_done, 1)
                    link(dve.tensor_scalar(s2g[par], s2, gt, None, ALU.mult), s2g_done, b + 1)
                if q.down:
                    for quarter in range(1, 4):
                        project_out(b - 1, quarter, 1 - par)

        @block.tensor
        def _(pe):
            def misc_wait(b, n):
                pe.wait_ge(misc_free, misc_use(b, n))

            def spread_s(b):
                pe.wait_ge(dgs_done, 2 * (b + 1))
                misc_wait(b, 0)
                pe.matmul(misc[:, 0:L], ones[:, :], dg[:, :, :], start=True, stop=True).then_inc(misc_full, 1)

            def transpose_input(b, t):
                pe.wait_ge(prep["q"], 2 * b + t + 1)
                misc_wait(b, 1 + t)
                for k in range(NK):
                    mm = pe.transpose(misc[:, :].bitcast(BF16)[:, k * P:(k + 1) * P],
                                      qrow[:, t, k * P:(k + 1) * P], identb[:, :])
                mm.then_inc(misc_full, 1)

            def down_project(b, quarter, par, first=0, end=NI):
                t, c = quarter // 2, quarter % 2
                if first == 0:
                    pe.wait_ge(y_done, 4 * b if quarter < 3 else 4 * b + 2)
                bk = down[DOWN_BANK[quarter]]
                for i in range(first, end):
                    if quarter == 0:
                        pe.wait_ge(q2_done, NI * b + i + 1)
                    n = rows(i)
                    mm = pe.matmul(bk[:, :], q2(par, i)[0:n, t, :],
                                   wdT[0:n, i, c * HALF:(c + 1) * HALF], start=(i == 0), stop=(i == NI - 1))
                if end == NI:
                    mm.then_inc(down_full, 1)

            pe.wait_ge(const_in, 48)
            pe.wait_ge(set_up, 4)
            pe.wait_ge(ident_done, 1)
            pe.wait_ge(scale_in, 64)
            for half in range(2):
                mm = pe.transpose(misc[:, half * NI:(half + 1) * NI], rb[0:NI, half * P:(half + 1) * P],
                                  identf[0:NI, 0:NI])
            mm.then_inc(misc_full, 1)
            spread_s(0)
            for t in range(2):
                transpose_input(0, t)
            for q in steps(pe):
                b, par = q.b, q.par
                if q.hidden:
                    pe.wait_ge(misc_free, misc_use(b, 2) + 1)
                    for i in range(NI):
                        n = rows(i)
                        if isinstance(b, int) and b == 0:
                            pe.wait_ge(gu_in[(i * P + n - 1) // PER], 32)
                        use, bk = q.use(i)
                        if not (isinstance(b, int) and b == 0 and i < RING):
                            pe.wait_ge(hid_done, use + 1 - RING)
                        for j, wT in enumerate((wgT, wuT)):
                            for k in range(NK):
                                mm = pe.matmul(bk[0:n, j, :], wT[:, k, i * P:i * P + n], qT[:, k, :],
                                               start=(k == 0), stop=(k == NK - 1))
                        mm.then_inc(gu_full, 1)
                if q.more:
                    spread_s(b + 1)
                if q.down:
                    pe.wait_ge(wd_in, 32)
                    down_project(b - 1, 0, 1 - par)
                if q.more:
                    transpose_input(b + 1, 0)
                if q.down:
                    down_project(b - 1, 1, 1 - par, 0, NI // 2)
                if q.more:
                    transpose_input(b + 1, 1)
                if q.down:
                    down_project(b - 1, 1, 1 - par, NI // 2, NI)
                if q.hidden:
                    pe.wait_ge(mx_done, NI * (b + 1))
                    misc_wait(b, 3)
                    for t in range(2):
                        mm = pe.transpose(misc[:, t * P:(t + 1) * P], mx[:, t * P:(t + 1) * P], identf[:, :])
                    mm.then_inc(misc_full, 1)
                if q.down:
                    down_project(b - 1, 2, 1 - par)
                if q.hidden:
                    pe.wait_ge(dgr_done, 2 * (b + 1))
                    misc_wait(b, 4)
                    pe.matmul(misc[:, 0:L], ones[:, :], dg[:, :, :], start=True, stop=True).then_inc(misc_full, 1)
                if q.down:
                    down_project(b - 1, 3, 1 - par)


def program(nc, io, out):
    B, L, D = io["x"].shape
    I = io["wg"].shape[0]

    def internal(name, shape, dt=F32):
        return nc.dram_tensor(name, shape, dt, kind="Internal").ap()

    scratch = {
        "x1": internal("x1", (B, L, D)),
        "ws_g": internal("ws_g", (I,)), "ws_u": internal("ws_u", (I,)), "ws_d": internal("ws_d", (D,)),
        "wT_g": internal("wT_g", (P, D // P, I), BF16), "wT_u": internal("wT_u", (P, D // P, I), BF16),
        "wT_d": internal("wT_d", (P, -(-I // P), D), BF16),
    }
    with ExitStack() as sems:
        attention_and_weights(nc, sems, io, scratch)
        feed_forward(nc, sems, io, scratch, out)


INPUTS = {"x": "x", "ctx": "ctx_4096", "g_x": "g_xattn", "g_f": "g_ffn", "w_rms": "L0_ffn_rmsnorm_weight",
          "wg": "L0_ffn_Wg", "wu": "L0_ffn_Wu", "wd": "L0_ffn_Wd"}


def kernel(**inputs):
    import numpy as np
    import concourse.bacc as bacc
    from concourse.bass_utils import run_bass_kernel_spmd

    nc = bacc.Bacc("TRN2", target_bir_lowering=False, num_devices=1)
    arrays = {f"in_{k}": np.ascontiguousarray(inputs[name]) for k, name in INPUTS.items()}
    arrays["in_const"] = dft_constants()
    io = {k[3:]: nc.dram_tensor(k, a.shape, mybir.dt.from_np(a.dtype), kind="ExternalInput").ap()
          for k, a in arrays.items()}
    out = nc.dram_tensor("out", inputs["x"].shape, F32, kind="ExternalOutput").ap()
    program(nc, io, out)
    result = run_bass_kernel_spmd(nc, [arrays], core_ids=[0])
    return result.results[0]["out"]
```
